# Optimizing a Trainium2 kernel written in Bass

```python
import numpy as np
import jax
import jax.numpy as jnp

def _softmax(x, axis=-1):
    return jax.nn.softmax(x, axis=axis)

def _gelu(x):
    return jax.nn.gelu(x, approximate=True)

def _silu(x):
    return jax.nn.silu(x)

def _sigmoid(x):
    return jax.nn.sigmoid(x)

def _layernorm(x, axis=-1, eps=1e-05):
    m = jnp.mean(x, axis=axis, keepdims=True)
    v = jnp.var(x, axis=axis, keepdims=True)
    return (x - m) / jnp.sqrt(v + eps)

def _scatter_add(tgt, idx, src, axis=0):
    return tgt.at[idx].add(src)

def _segment_sum(src, seg, n):
    return jax.ops.segment_sum(src, seg, n)
kernel_name = 'mk_gnn_resnorm_d1_gnn_r8_da2d11'

def setup_inputs(seed: int=0):
    np.random.seed(seed)
    _w = jnp.asarray

    def _rec_inputs():
        import jax
        import jax.numpy as jnp
        _gk = jax.random.key(seed)
        x = -0.000202 + 1 * jax.random.normal(jax.random.fold_in(_gk, 1), (6250, 128), jnp.float32)
        src = jax.random.randint(jax.random.fold_in(_gk, 2), (100000,), 0, 6250, jnp.int32)
        dst = jnp.minimum((6250 * jax.random.uniform(jax.random.fold_in(_gk, 3), (100000,)) ** 2.0).astype(jnp.int32), 49999)
        _o = jnp.argsort(dst, stable=True)
        src = src[_o]
        dst = dst[_o]
        return (x, src, dst)
    x, src, dst = _rec_inputs()

    def _L0_gnn_setup():
        import jax, jax.numpy as jnp
        import numpy as np
        N_NODES, N_EDGES = (6250, 100000)
        NODE_D, MSG_D, OUT_D = (128, 128, 128)

        def _linear_params(key, d_in, d_out):
            kw, _ = jax.random.split(key)
            W = jax.random.normal(kw, (d_in, d_out), jnp.float32) * np.float32(1.0 / np.sqrt(d_in))
            b = jnp.zeros((d_out,), jnp.float32)
            return (W, b)
        key = jax.random.key(seed)
        ks = jax.random.split(key, 12)
        node_features = jax.random.normal(ks[0], (N_NODES, NODE_D), jnp.float32)
        src = jax.random.randint(ks[1], (N_EDGES,), 0, N_NODES, dtype=jnp.int32)
        dst = jax.random.randint(ks[2], (N_EDGES,), 0, N_NODES, dtype=jnp.int32)
        W_msg_1, b_msg_1 = _linear_params(ks[3], NODE_D, MSG_D)
        W_msg_2, b_msg_2 = _linear_params(ks[4], MSG_D, MSG_D)
        W_msg_3, b_msg_3 = _linear_params(ks[5], MSG_D, MSG_D)
        W_att_1, b_att_1 = _linear_params(ks[6], 2 * NODE_D, 1)
        W_att_2, b_att_2 = _linear_params(ks[7], 2 * NODE_D, 1)
        W_att_3, b_att_3 = _linear_params(ks[8], 2 * NODE_D, 1)
        W_c1, b_c1 = _linear_params(ks[9], MSG_D + NODE_D, OUT_D)
        W_c2, b_c2 = _linear_params(ks[10], OUT_D, OUT_D)
        return {'node_features': node_features, 'src': src, 'dst': dst, 'W_msg_1': W_msg_1, 'b_msg_1': b_msg_1, 'W_msg_2': W_msg_2, 'b_msg_2': b_msg_2, 'W_msg_3': W_msg_3, 'b_msg_3': b_msg_3, 'W_att_1': W_att_1, 'b_att_1': b_att_1, 'W_att_2': W_att_2, 'b_att_2': b_att_2, 'W_att_3': W_att_3, 'b_att_3': b_att_3, 'W_c1': W_c1, 'b_c1': b_c1, 'W_c2': W_c2, 'b_c2': b_c2}
    _L0_gnn_all = _L0_gnn_setup()
    _L0_gnn_in = {k: v for k, v in _L0_gnn_all.items() if k in ('W_msg_1', 'b_msg_1', 'W_msg_2', 'b_msg_2', 'W_msg_3', 'b_msg_3', 'W_att_1', 'b_att_1', 'W_att_2', 'b_att_2', 'W_att_3', 'b_att_3', 'W_c1', 'b_c1', 'W_c2', 'b_c2')}
    del _L0_gnn_all
    return {'x': x, 'src': src, 'dst': dst, 'L0_gnn_W_msg_1': _L0_gnn_in['W_msg_1'], 'L0_gnn_b_msg_1': _L0_gnn_in['b_msg_1'], 'L0_gnn_W_msg_2': _L0_gnn_in['W_msg_2'], 'L0_gnn_b_msg_2': _L0_gnn_in['b_msg_2'], 'L0_gnn_W_msg_3': _L0_gnn_in['W_msg_3'], 'L0_gnn_b_msg_3': _L0_gnn_in['b_msg_3'], 'L0_gnn_W_att_1': _L0_gnn_in['W_att_1'], 'L0_gnn_b_att_1': _L0_gnn_in['b_att_1'], 'L0_gnn_W_att_2': _L0_gnn_in['W_att_2'], 'L0_gnn_b_att_2': _L0_gnn_in['b_att_2'], 'L0_gnn_W_att_3': _L0_gnn_in['W_att_3'], 'L0_gnn_b_att_3': _L0_gnn_in['b_att_3'], 'L0_gnn_W_c1': _L0_gnn_in['W_c1'], 'L0_gnn_b_c1': _L0_gnn_in['b_c1'], 'L0_gnn_W_c2': _L0_gnn_in['W_c2'], 'L0_gnn_b_c2': _L0_gnn_in['b_c2']}

def reference(x, src, dst, L0_gnn_W_msg_1, L0_gnn_b_msg_1, L0_gnn_W_msg_2, L0_gnn_b_msg_2, L0_gnn_W_msg_3, L0_gnn_b_msg_3, L0_gnn_W_att_1, L0_gnn_b_att_1, L0_gnn_W_att_2, L0_gnn_b_att_2, L0_gnn_W_att_3, L0_gnn_b_att_3, L0_gnn_W_c1, L0_gnn_b_c1, L0_gnn_W_c2, L0_gnn_b_c2):
    import jax
    import jax.numpy as jnp

    def _L0_gnn_ref(node_features, src, dst, W_msg_1, b_msg_1, W_msg_2, b_msg_2, W_msg_3, b_msg_3, W_att_1, b_att_1, W_att_2, b_att_2, W_att_3, b_att_3, W_c1, b_c1, W_c2, b_c2):
        import jax, jax.numpy as jnp
        import numpy as np
        N_NODES, N_EDGES = (6250, 100000)
        NODE_D, MSG_D, OUT_D = (128, 128, 128)

        def _linear_params(key, d_in, d_out):
            kw, _ = jax.random.split(key)
            W = jax.random.normal(kw, (d_in, d_out), jnp.float32) * np.float32(1.0 / np.sqrt(d_in))
            b = jnp.zeros((d_out,), jnp.float32)
            return (W, b)
        h = node_features
        N = h.shape[0]
        hs = h[src]
        hd = h[dst]
        e = jnp.concatenate([hs, hd], axis=1)
        a1 = jnp.exp(jax.nn.relu(e @ W_att_1 + b_att_1))
        a2 = jnp.exp(jax.nn.relu(e @ W_att_2 + b_att_2))
        a3 = jnp.exp(jax.nn.relu(e @ W_att_3 + b_att_3))
        att1 = jax.ops.segment_sum(a1, dst, num_segments=N)
        att2 = jax.ops.segment_sum(a2, dst, num_segments=N)
        att3 = jax.ops.segment_sum(a3, dst, num_segments=N)
        avg_a = (a1 / att1[dst] + a2 / att2[dst] + a3 / att3[dst]) / 3.0
        m = avg_a * jax.nn.relu(jax.nn.relu(jax.nn.relu(hs @ W_msg_1 + b_msg_1) @ W_msg_2 + b_msg_2) @ W_msg_3 + b_msg_3)
        deg = jax.ops.segment_sum(jnp.ones((src.shape[0], 1), h.dtype), dst, num_segments=N)
        h_neigh = jax.ops.segment_sum(m, dst, num_segments=N) / jnp.maximum(deg, 1.0)
        hc = jnp.concatenate([h, h_neigh], axis=1)
        out = jax.nn.relu(hc @ W_c1 + b_c1) @ W_c2 + b_c2
        return out
    x = _layernorm(x + _L0_gnn_ref(x, src, dst, L0_gnn_W_msg_1, L0_gnn_b_msg_1, L0_gnn_W_msg_2, L0_gnn_b_msg_2, L0_gnn_W_msg_3, L0_gnn_b_msg_3, L0_gnn_W_att_1, L0_gnn_b_att_1, L0_gnn_W_att_2, L0_gnn_b_att_2, L0_gnn_W_att_3, L0_gnn_b_att_3, L0_gnn_W_c1, L0_gnn_b_c1, L0_gnn_W_c2, L0_gnn_b_c2), axis=-1)
    return x

_drawn_inputs = setup_inputs


def setup_inputs(seed=0):
    import zlib

    import numpy as np

    out = dict(_drawn_inputs(seed))
    spreads = {'L0_gnn_b_msg_1': (0.0, 0.8),
     'L0_gnn_b_msg_2': (0.0, 2.0),
     'L0_gnn_b_msg_3': (0.0, 2.0),
     'L0_gnn_b_c1': (0.0, 0.395),
     'L0_gnn_b_c2': (0.0, 0.305)}
    factors = {'L0_gnn_W_msg_1': 8.0,
     'L0_gnn_W_msg_2': 7.931,
     'L0_gnn_W_msg_3': 4.98,
     'L0_gnn_W_att_1': 8.0,
     'L0_gnn_W_att_2': 8.0,
     'L0_gnn_W_att_3': 8.0}
    for name, (base, spread) in spreads.items():
        noise = np.random.default_rng([zlib.crc32(name.encode()), seed]).standard_normal(out[name].shape)
        drawn = base * np.exp(spread * noise) if base else spread * noise
        out[name] = jnp.asarray(drawn.astype(out[name].dtype))
    for name, factor in factors.items():
        out[name] = (out[name] * factor).astype(out[name].dtype)
    return out
```

```python
import concourse.bass as bass
import concourse.mybir as mybir
from contextlib import ExitStack

P = 128
HEADS = 3
WIN = 48
TILES = 2
GROUP = TILES * P
ROW = P + HEADS
CHUNK = 4
COLS = CHUNK * P
DONE = float(1 << 20)
FLT_MAX = 3.4028234663852886e38
EPS = 1e-5

RING = 8
N_EXP = 3
N_WT = 4
N_SUM = 3
N_QW = 2
REGS = 16


def gnn_program(nc, x, src, dst, w_msg, b_msg, w_att, b_att, w_c1, b_c1, w_c2, b_c2, table, out):
    f32, bf16, i32 = mybir.dt.float32, mybir.dt.bfloat16, mybir.dt.int32
    ALU, ACT, AX = mybir.AluOpType, mybir.ActivationFunctionType, mybir.AxisListType.X

    n_nodes = x.shape[0]
    n_edges = src.shape[0]
    n_blocks = -(-n_nodes // P)
    n_cols = n_blocks * P
    n_pad = -(-max(n_cols, n_nodes + WIN) // 32) * 32
    n_chunks = -(-n_blocks // CHUNK)
    n_groups = -(-n_edges // GROUP)
    n_rows = -(-n_groups // P)
    full_groups = n_edges // GROUP
    tail_edges = n_edges - full_groups * GROUP

    def blocks_of(c):
        return min(CHUNK, n_blocks - c * CHUNK)

    def nodes_of(c):
        return min(COLS, n_nodes - c * COLS)

    def block_nodes(i):
        return min(P, n_nodes - i * P)

    def tile_edges(g, h):
        return min(P, n_edges - g * GROUP - h * P)

    ctx = ExitStack()
    with ctx:
        def sb(name, shape, dt=f32):
            return ctx.enter_context(nc.sbuf_tensor(name, shape, dt))

        def sem(name):
            return ctx.enter_context(nc.semaphore(name))

        x_rows = sb("x_rows", [P, n_blocks, P])
        x_t = sb("x_t", [P, n_cols])
        acc = sb("acc", [P, HEADS + 1, n_pad])
        split = sb("split", [3 * HEADS, n_pad], bf16)
        w1 = sb("w1", [P, P])
        w2 = sb("w2", [P, P])
        w3 = sb("w3", [P, P])
        wc1 = sb("wc1", [P, 2, P])
        wc2 = sb("wc2", [P, P])
        w_logit = sb("w_logit", [P, 2 * HEADS])
        b1 = sb("b1", [P, 1])
        b2 = sb("b2", [P, 1])
        bc1 = sb("bc1", [P, 1])
        b3_all = sb("b3_all", [P, P])
        bc2_all = sb("bc2_all", [P, P])
        b_logit = sb("b_logit", [P, HEADS])
        ident = sb("ident", [P, P])
        ident_bf = sb("ident_bf", [P, P], bf16)
        pick = sb("pick", [3 * HEADS, HEADS, P], bf16)
        columns = sb("columns", [P, WIN])
        columns_i = sb("columns_i", [P, WIN], i32)
        per_node = sb("per_node", [P, n_blocks, 4])
        part_rest = sb("part_rest", [P, n_blocks, HEADS])
        parts = sb("parts", [P, n_blocks, 3 * HEADS], bf16)
        eps_col = sb("eps_col", [P, 1])

        n_ids = 2 * n_rows * GROUP
        ids_i = acc[:, HEADS, 0:n_ids].bitcast(i32).rearrange("p (j r e) -> p j r e", j=2, e=GROUP)
        dst_left = sb("dst_left", [P, n_rows, GROUP])
        src_t = sb("src_t", [P, TILES, n_rows * P], i32)
        dst_t = sb("dst_t", [P, TILES, n_rows * P])
        win_row = sb("win_row", [1, n_rows * P], i32)
        win_col = sb("win_col", [P, n_rows])
        least = sb("least", [P, 1])
        least_all = sb("least_all", [1, 1])
        more = sb("more", [1, 1], i32)

        WORK = 5400
        work = sb("work", [P, WORK])

        def area(at, *dims):
            n = 1
            for d in dims:
                n *= d
            view = work[:, at:at + n]
            if len(dims) == 2:
                view = view.rearrange("p (a b) -> p a b", a=dims[0])
            if len(dims) == 3:
                view = view.rearrange("p (a b c) -> p a b c", a=dims[0], b=dims[1])
            if len(dims) == 4:
                view = view.rearrange("p (a b c d) -> p a b c d", a=dims[0], b=dims[1], c=dims[2])
            return view, at + n

        bank = [ctx.enter_context(nc.psum_tensor(f"bank{i}", [P, 512], f32)) for i in range(8)]

        def bank_bf(i):
            return bank[i][:, :].bitcast(bf16)

        h1, at = area(0, 2, COLS)
        h2, at = area(at, 2, COLS)
        msg, at = area(at, 2, CHUNK, P)
        rows, at = area(at, 2, CHUNK, ROW)
        src_f, _ = area(0, n_rows, GROUP)
        assert at <= WORK

        def src_bank(h):
            return bank[h]

        n_weight_dmas = 4 + 1 + 3 + 2 + 3 * HEADS
        n_id_dmas = 2 * (full_groups // P + (full_groups % P > 0) + (tail_edges > 0))

        s_w = sem("s_w")
        s_x = [sem(f"s_x{c}") for c in range(n_chunks)]
        s_ids = sem("s_ids")
        s_idz = sem("s_idz")
        s_const = sem("s_const")
        s_cdve = sem("s_cdve")
        s_tr = sem("s_tr")
        s_xt = sem("s_xt")
        s_l1 = sem("s_l1")
        s_h1 = sem("s_h1")
        s_l2 = sem("s_l2")
        s_h2 = sem("s_h2")
        s_l3 = sem("s_l3")
        s_msg = sem("s_msg")
        s_pq = sem("s_pq")
        s_row = sem("s_row")
        s_xb = sem("s_xb")
        s_tab = [sem(f"s_tab{j}") for j in range(2)]
        s_d1 = sem("s_d1")
        s_pt = sem("s_pt")
        s_pc = sem("s_pc")
        s_st = sem("s_st")

        BF_COLS = 1024
        n_part_banks = -(-n_cols // BF_COLS)

        def transpose_parts(pe, wait_for):
            pe.wait_ge(*wait_for)
            for b in range(n_part_banks):
                blocks = range(b * 8, min(b * 8 + 8, n_blocks))
                for i in blocks:
                    last = pe.transpose(bank_bf(b)[0:3 * HEADS, (i - b * 8) * P:(i - b * 8 + 1) * P],
                                        parts[:, i, :], ident_bf[:, :])
                last.then_inc(s_pt_now[0], 1)

        s_pt_now = [s_pt]

        def copy_parts(act, done):
            for b in range(n_part_banks):
                n = min(BF_COLS, n_cols - b * BF_COLS)
                act.wait_ge(s_pt_now[0], b + 1)
                act.copy(split[:, b * BF_COLS:b * BF_COLS + n],
                         bank_bf(b)[0:3 * HEADS, 0:n]).then_inc(done, 1)

        def split_parts(dve, chain):
            value = per_node[:, :, 0:HEADS]
            for j in range(3):
                part = parts[:, :, j * HEADS:(j + 1) * HEADS]
                chain(dve.tensor_copy(part, value))
                if j < 2:
                    chain(dve.tensor_tensor(part_rest[:, :, :], value, part, ALU.subtract))
                    value = part_rest[:, :, :]

        def chained(eng, s):
            count = [0]

            def chain(instruction):
                count[0] += 1
                instruction.then_inc(s, 1)
                eng.wait_ge(s, count[0])
                return count[0]
            return chain

        with nc.Block() as block:
            @block.sync
            def _(sp):
                sp.dma_start(w1[:, :], w_msg[0]).then_inc(s_w, 16)
                for c in range(n_chunks):
                    n = nodes_of(c)
                    if n == COLS:
                        to = x_rows[:, c * CHUNK:(c + 1) * CHUNK, :]
                        of = x[c * COLS:(c + 1) * COLS, :].rearrange("(i p) f -> p i f", p=P)
                    else:
                        assert n <= P
                        to, of = x_rows[0:n, c * CHUNK, :], x[c * COLS:n_nodes, :]
                    sp.dma_start(to, of).then_inc(s_x[c], 16)
                for c in range(n_chunks):
                    n = nodes_of(c)
                    sp.wait_ge(s_row, c + 1)
                    if n == COLS:
                        to = table[c * COLS:(c + 1) * COLS, :].rearrange("(i p) f -> p i f", p=P)
                        of = rows[:, c % 2, :, :]
                    else:
                        to, of = table[c * COLS:n_nodes, :], rows[0:n, c % 2, 0, :]
                    sp.dma_start(to, of).then_inc(s_tab[c % 2], 16)
                for j in range(2):
                    sp.wait_ge(s_tab[j], 16 * len(range(j, n_chunks, 2)))

            @block.scalar
            def _(act):
                loads = [(w2, w_msg[1]), (w3, w_msg[2]), (wc2, w_c2)]
                for to, of in loads:
                    act.dma_start(to[:, :], of).then_inc(s_w, 16)
                act.dma_start(wc1[:, :, :], w_c1.rearrange("(h p) f -> p h f", p=P)).then_inc(s_w, 16)
                for to, of in ((b1, b_msg[0]), (b2, b_msg[1]), (bc1, b_c1)):
                    act.dma_start(to[:, :], of.rearrange("(p o) -> p o", o=1)).then_inc(s_w, 16)
                for to, of in ((b3_all, b_msg[2]), (bc2_all, b_c2)):
                    act.dma_start(to[:, :], of.partition_broadcast(P)).then_inc(s_w, 16)
                for k in range(HEADS):
                    for h in range(2):
                        act.dma_start(w_logit[:, h * HEADS + k:h * HEADS + k + 1],
                                      w_att[k][h * P:(h + 1) * P, :]).then_inc(s_w, 16)
                    act.dma_start(b_logit[:, k:k + 1], b_att[k].partition_broadcast(P)).then_inc(s_w, 16)
                act.wait_ge(s_idz, 2)
                for j, ids in enumerate((src, dst)):
                    r, done = 0, 0
                    for r in range(full_groups // P):
                        act.dma_start(ids_i[:, j, r, :],
                                      ids[r * P * GROUP:(r + 1) * P * GROUP].rearrange("(p e) -> p e", e=GROUP)
                                      ).then_inc(s_ids, 16)
                        done = (r + 1) * P
                    left = full_groups - done
                    if left:
                        act.dma_start(ids_i[0:left, j, done // P, :],
                                      ids[done * GROUP:full_groups * GROUP].rearrange("(p e) -> p e", e=GROUP)
                                      ).then_inc(s_ids, 16)
                    if tail_edges:
                        p, r = full_groups % P, full_groups // P
                        act.dma_start(ids_i[p:p + 1, j, r, 0:tail_edges],
                                      ids[full_groups * GROUP:n_edges].rearrange("(p e) -> p e", p=1)
                                      ).then_inc(s_ids, 16)
                act.wait_ge(s_w, 16 * n_weight_dmas)
                for c in range(n_chunks + 1):
                    if c < n_chunks:
                        n = nodes_of(c)
                        act.wait_ge(s_tr, c + 1)
                        act.copy(x_t[:, c * COLS:c * COLS + n], bank[c % 2][:, 0:n]).then_inc(s_xt, 1)
                    if c >= 1:
                        n = nodes_of(c - 1)
                        act.wait_ge(s_l1, c)
                        if c >= 3:
                            act.wait_ge(s_l2, c - 2)
                        act.activation(h1[:, (c - 1) % 2, 0:n], bank[2][:, 0:n], ACT.Relu,
                                       bias=b1[:, 0:1]).then_inc(s_h1, 1)
                copy_parts(act, s_pc)

            @block.vector
            def _(dve):
                chain = chained(dve, s_cdve)
                dve.memset(eps_col[:, :], EPS)
                dve.memset(per_node[:, :, :], 0.0)
                dve.memset(split[:, n_cols:n_pad], 0.0)
                dve.memset(x_t[:, n_nodes:n_cols], 0.0)
                step = -(-HEADS * n_pad // n_chunks)
                acc_flat = acc[:, 0:HEADS, :].rearrange("p k n -> p (k n)")
                dve.memset(acc[:, HEADS, n_ids:n_pad], 0.0)
                dve.wait_ge(s_const, 6)
                chain(dve.tensor_copy(ident_bf[:, :], ident[:, :]))
                chain(dve.tensor_copy(columns[:, :], columns_i[:, :]))
                dve.wait_ge(s_w, 16 * n_weight_dmas)
                for c in range(n_chunks + 1):
                    if c < n_chunks:
                        n = nodes_of(c)
                        dve.wait_ge(s_l2, c + 1)
                        if c >= 2:
                            dve.wait_ge(s_l3, c - 1)
                        dve.tensor_scalar(h2[:, c % 2, 0:n], bank[3][:, 0:n], b2[:, 0:1], 0.0,
                                          ALU.add, ALU.max).then_inc(s_h2, 1)
                        lo, hi = c * step, min((c + 1) * step, HEADS * n_pad)
                        dve.memset(acc_flat[:, lo:hi], 0.0)
                    if c >= 1:
                        d = c - 1
                        nb, m = blocks_of(d), min(nodes_of(d), P)
                        dve.wait_ge(s_l3, d + 1)
                        if d >= 2:
                            dve.wait_ge(s_row, d - 1)
                            dve.wait_ge(s_tab[d % 2], 16 * (d // 2))
                        dve.tensor_tensor(msg[0:m, d % 2, 0:nb, :],
                                          bank[4 + d % 2][0:m, 0:nb * P].rearrange("p (i f) -> p i f", f=P),
                                          b3_all[0:m, :].unsqueeze(1).to_broadcast([m, nb, P]),
                                          ALU.add).then_inc(s_msg, 1)
                        logits = bank[6 + d % 2][0:m, 0:nb * 6].rearrange("p (i j) -> p i j", j=6)
                        dve.tensor_copy(rows[0:m, d % 2, 0:nb, P:ROW], logits[:, :, 0:HEADS])
                        dve.tensor_tensor(per_node[0:m, d * CHUNK:d * CHUNK + nb, 0:HEADS],
                                          logits[:, :, HEADS:2 * HEADS],
                                          b_logit[0:m, :].unsqueeze(1).to_broadcast([m, nb, HEADS]),
                                          ALU.add).then_inc(s_pq, 1)
                dve.wait_ge(s_pq, n_chunks)
                chain = chained(dve, s_d1)
                split_parts(dve, chain)
                dve.wait_ge(s_ids, 16 * n_id_dmas)
                chain(dve.tensor_copy(dst_left[:, :, :], ids_i[:, 1, :, :]))
                dve.wait_ge(s_tab[0], 16 * len(range(0, n_chunks, 2)))
                dve.wait_ge(s_tab[1], 16 * len(range(1, n_chunks, 2)))
                chain(dve.tensor_copy(src_f, ids_i[:, 0, :, :]))
                dve.memset(acc[:, HEADS, 0:n_ids], 0.0)
                dve.wait_ge(s_st, 1)
                for h in range(TILES):
                    dve.tensor_copy(src_t[:, h, :], src_bank(h)[:, 0:n_rows * P])

            @block.gpsimd
            def _(pool):
                pool.memset(ids_i[:, 0, :, :], 0).then_inc(s_idz, 1)
                pool.memset(ids_i[:, 1, :, :], int(DONE)).then_inc(s_idz, 1)
                pool.memset(ident[:, :], 0.0).then_inc(s_const, 1)
                pool.memset(pick[:, :, :], 0.0).then_inc(s_const, 1)
                pool.iota(columns_i[:, :], pattern=[[1, WIN]], base=0,
                          channel_multiplier=0).then_inc(s_const, 1)
                pool.wait_ge(s_const, 3)
                pool.affine_select(out=ident[:, :], in_=ident[:, :], compare_op=ALU.not_equal, fill=1.0,
                                   base=0, pattern=[[-1, P]], channel_multiplier=1).then_inc(s_const, 1)
                for part in range(3):
                    pool.affine_select(out=pick[:, :, :], in_=pick[:, :, :], compare_op=ALU.not_equal,
                                       fill=1.0, base=-HEADS * part, pattern=[[-1, HEADS], [0, P]],
                                       channel_multiplier=1).then_inc(s_const, 1)
                    pool.wait_ge(s_const, 5 + part)
                pool.wait_ge(s_w, 16 * n_weight_dmas)
                for c in range(n_chunks):
                    nb, m = blocks_of(c), min(nodes_of(c), P)
                    pool.wait_ge(s_tr, c + 1)
                    pool.tensor_tensor(x_rows[0:m, c * CHUNK:c * CHUNK + nb, :],
                                       x_rows[0:m, c * CHUNK:c * CHUNK + nb, :],
                                       bc2_all[0:m, :].unsqueeze(1).to_broadcast([m, nb, P]),
                                       ALU.add).then_inc(s_xb, 1)
                    pool.wait_ge(s_pq, c + 1)
                    pool.tensor_scalar_max(rows[0:m, c % 2, 0:nb, 0:P], msg[0:m, c % 2, 0:nb, :],
                                           0.0).then_inc(s_row, 1)

            @block.tensor
            def _(pe):
                pe.wait_ge(s_const, 4)
                pe.wait_ge(s_w, 16 * n_weight_dmas)
                for s in range(n_chunks + 3):
                    if s < n_chunks:
                        c = s
                        pe.wait_ge(s_x[c], 16)
                        if c >= 2:
                            pe.wait_ge(s_xt, c - 1)
                        for i in range(blocks_of(c)):
                            m = block_nodes(c * CHUNK + i)
                            last = pe.transpose(bank[c % 2][:, i * P:i * P + m],
                                                x_rows[0:m, c * CHUNK + i, :], ident[0:m, 0:m])
                        last.then_inc(s_tr, 1)
                    if 0 <= s - 1 < n_chunks:
                        c, n = s - 1, nodes_of(s - 1)
                        pe.wait_ge(s_xt, c + 1)
                        if c >= 1:
                            pe.wait_ge(s_h1, c)
                        pe.matmul(bank[2][:, 0:n], w1[:, :], x_t[:, c * COLS:c * COLS + n],
                                  start=True, stop=True).then_inc(s_l1, 1)
                    if 0 <= s - 2 < n_chunks:
                        c, n = s - 2, nodes_of(s - 2)
                        pe.wait_ge(s_h1, c + 1)
                        if c >= 1:
                            pe.wait_ge(s_h2, c)
                        pe.matmul(bank[3][:, 0:n], w2[:, :], h1[:, c % 2, 0:n],
                                  start=True, stop=True).then_inc(s_l2, 1)
                    if 0 <= s - 3 < n_chunks:
                        c = s - 3
                        pe.wait_ge(s_h2, c + 1)
                        if c >= 2:
                            pe.wait_ge(s_pq, c - 1)
                        for i in range(blocks_of(c)):
                            b = c * CHUNK + i
                            m = block_nodes(b)
                            pe.matmul(bank[4 + c % 2][0:m, i * P:(i + 1) * P],
                                      h2[:, c % 2, i * P:i * P + m], w3[:, :], start=True, stop=True)
                            last = pe.matmul(bank[6 + c % 2][0:m, i * 6:(i + 1) * 6],
                                             x_t[:, b * P:b * P + m], w_logit[:, :], start=True, stop=True)
                        last.then_inc(s_l3, 1)
                pe.wait_ge(s_pq, n_chunks)
                pe.wait_ge(s_cdve, 1)
                transpose_parts(pe, (s_d1, 5))
                pe.wait_ge(s_pc, n_part_banks)
                pe.wait_ge(s_d1, 7)
                for h in range(TILES):
                    for r in range(n_rows):
                        last = pe.transpose(src_bank(h)[:, r * P:(r + 1) * P],
                                            src_f[:, r, h * P:(h + 1) * P], ident[:, :])
                last.then_inc(s_st, 1)

        nc.all_engine_barrier()

        dist, at = area(0, n_rows, GROUP)
        hit, at = area(at, n_rows, GROUP)
        assert at <= WORK
        gath, at = area(0, RING * TILES, ROW)
        expo, at = area(at, N_EXP, HEADS + 1, TILES * WIN)
        mask, at = area(at, N_EXP, TILES, WIN)
        wt, at = area(at, N_WT, HEADS + 1, TILES * WIN)
        a_sum, at = area(at, N_WT, TILES, HEADS + 1)
        assert at <= WORK

        s_first = sem("s_first")
        s_prep = sem("s_prep")
        s_ptr = sem("s_ptr")
        s_gath = [sem(f"s_gath{j}") for j in range(RING * TILES)]
        s_fill = sem("s_fill")
        s_qw = sem("s_qw")
        s_exp = sem("s_exp")
        s_mask = sem("s_mask")
        s_wt = sem("s_wt")
        s_as = sem("s_as")
        s_sum = sem("s_sum")
        s_acc = sem("s_acc")
        s_last = sem("s_last")

        more_reg = nc.alloc_registers("more")
        nc.br("pass_start")
        with nc.body("pass_start", valid_engines=mybir.ALL_ENGINES):
            with nc.Block() as block:
                @block.vector
                def _(dve):
                    chain = chained(dve, s_prep)
                    chain(dve.tensor_reduce(win_col[:, :], dst_left[:, :, :], AX, ALU.min))
                    chain(dve.tensor_scalar_min(win_col[:, :], win_col[:, :], float(n_nodes)))
                    chain(dve.tensor_tensor(dist[:, :, :], dst_left[:, :, :],
                                            win_col[:, :].unsqueeze(2).to_broadcast([P, n_rows, GROUP]),
                                            ALU.subtract))
                    chain(dve.tensor_scalar(hit[:, :, :], dist[:, :, :], float(WIN), DONE,
                                            ALU.is_lt, ALU.mult))
                    chain(dve.tensor_tensor(dst_left[:, :, :], dst_left[:, :, :], hit[:, :, :], ALU.add))
                    chain(dve.tensor_reduce(least[:, :], dst_left[:, :, :].rearrange("p r e -> p (r e)"),
                                            AX, ALU.min))
                    dve.wait_ge(s_ptr, 1)
                    for h in range(TILES):
                        dve.tensor_copy(dst_t[:, h, :], bank[h][:, 0:n_rows * P])
                    dve.wait_ge(s_ptr, 2)
                    dve.tensor_copy(win_row[0:1, :], bank[2][0:1, 0:n_rows * P])
                    chain(dve.tensor_reduce(least_all[:, :], bank[3][0:1, 0:P], AX, ALU.min))
                    chain(dve.tensor_scalar(more[:, :], least_all[:, :], DONE, None, ALU.is_lt))

                @block.tensor
                def _(pe):
                    pe.wait_ge(s_prep, 3)
                    for h in range(TILES):
                        for r in range(n_rows):
                            last = pe.transpose(bank[h][:, r * P:(r + 1) * P],
                                                dist[:, r, h * P:(h + 1) * P], ident[:, :])
                    last.then_inc(s_ptr, 1)
                    for r in range(n_rows):
                        pe.transpose(bank[2][0:1, r * P:(r + 1) * P], win_col[:, r:r + 1], ident[:, :])
                    pe.wait_ge(s_prep, 6)
                    pe.transpose(bank[3][0:1, 0:P], least[:, :], ident[:, :]).then_inc(s_ptr, 1)

            nc.all_engine_barrier()

            with nc.Block() as block:
                def window_registers(eng):
                    regs = {}

                    def window(g):
                        if g % REGS == 0:
                            n = min(REGS, n_groups - g)
                            fresh = [eng.alloc_register(f"win{g + j}") for j in range(n)]
                            eng.load(fresh, win_row[0:1, g:g + n])
                            for j in range(n):
                                regs[g + j] = eng.snap(fresh[j], donate=True, min_val=0, max_val=n_nodes)
                        return regs.pop(g)
                    return window

                @block.gpsimd
                def _(pool):
                    for g in range(n_groups):
                        if g >= RING:
                            pool.wait_ge(s_sum, g - RING + 1)
                        for h in range(TILES):
                            m = tile_edges(g, h)
                            slot = (g % RING) * TILES + h
                            pool.indirect_dma_start(
                                out=gath[0:m, slot, :], out_offset=None, in_=table[:, :],
                                in_offset=bass.IndirectOffsetOnAxis(ap=src_t[0:m, h, g:g + 1], axis=0),
                            ).then_inc(s_gath[slot], 16)

                def rows_landed(eng, g, h):
                    eng.wait_ge(s_gath[(g % RING) * TILES + h], 16 * (g // RING + 1))

                @block.tensor
                def _(pe):
                    window = window_registers(pe)

                    def q_window(g):
                        start = window(g)
                        if g >= N_QW:
                            pe.wait_ge(s_exp, g - N_QW + 1)
                        for k in range(HEADS):
                            last = pe.matmul(bank[g % N_QW][:, k * WIN:(k + 1) * WIN], pick[:, k, :],
                                             split[:, bass.ds(start, WIN)], start=True, stop=True)
                        last.then_inc(s_qw, 1)

                    for g in range(N_QW):
                        q_window(g)
                    pe.wait_ge(s_fill, 1)
                    for g in range(n_groups):
                        sums = bank[N_QW + g % N_SUM]
                        tiles = [h for h in range(TILES) if tile_edges(g, h) > 0]
                        pe.wait_ge(s_wt, g + 1)
                        if g >= N_SUM:
                            pe.wait_ge(s_acc, g - N_SUM + 1)
                        for h in tiles:
                            m = tile_edges(g, h)
                            rows_landed(pe, g, h)
                            pe.matmul(sums[:, 0:HEADS * WIN],
                                      gath[0:m, (g % RING) * TILES + h, 0:P],
                                      wt[0:m, g % N_WT, 0:HEADS, h * WIN:(h + 1) * WIN],
                                      start=h == tiles[0], stop=h == tiles[-1])
                        pe.wait_ge(s_as, g + 1)
                        for h in tiles:
                            m = tile_edges(g, h)
                            last = pe.matmul(sums[0:HEADS + 1, HEADS * WIN:(HEADS + 1) * WIN],
                                             a_sum[0:m, g % N_WT, h, :],
                                             wt[0:m, g % N_WT, HEADS, h * WIN:(h + 1) * WIN],
                                             start=h == tiles[0], stop=h == tiles[-1])
                        last.then_inc(s_sum, 1)
                        if g + N_QW < n_groups:
                            q_window(g + N_QW)

                @block.scalar
                def _(act):
                    for g in range(n_groups):
                        act.wait_ge(s_qw, g + 1)
                        if g >= N_EXP:
                            act.wait_ge(s_wt, g - N_EXP + 1)
                        for h in range(TILES):
                            m = tile_edges(g, h)
                            rows_landed(act, g, h)
                            slot = (g % RING) * TILES + h
                            for k in range(HEADS):
                                last = act.activation(expo[0:m, g % N_EXP, k, h * WIN:(h + 1) * WIN],
                                                      bank[g % N_QW][0:m, k * WIN:(k + 1) * WIN], ACT.Exp,
                                                      bias=gath[0:m, slot, P + k:P + k + 1])
                        last.then_inc(s_exp, 1)

                @block.vector
                def _(dve):
                    for j in range(N_EXP):
                        dve.memset(expo[:, j, HEADS, :], 0.0)
                    dve.memset(a_sum[:, :, :, :], 1.0)
                    for j in range(N_SUM):
                        last = dve.memset(bank[N_QW + j][:, HEADS * WIN:(HEADS + 1) * WIN], 0.0)
                    last.then_inc(s_fill, 1)
                    dve.wait_ge(s_fill, 1)
                    window = window_registers(dve)

                    def masks(g):
                        if g >= N_EXP:
                            dve.wait_ge(s_wt, g - N_EXP + 1)
                        for h in range(TILES):
                            last = dve.tensor_scalar(mask[:, g % N_EXP, h, :], columns[:, :],
                                                     dst_t[:, h, g:g + 1], FLT_MAX, ALU.is_equal, ALU.mult)
                        last.then_inc(s_mask, 1)

                    def add_sums(g):
                        start = window(g)
                        dve.wait_ge(s_sum, g + 1)
                        if g >= 1:
                            dve.wait_ge(s_acc, g)
                        here = acc[:, :, bass.ds(start, WIN)]
                        dve.tensor_tensor(here, here,
                                          bank[N_QW + g % N_SUM][:, 0:(HEADS + 1) * WIN].rearrange(
                                              "p (k w) -> p k w", w=WIN), ALU.add).then_inc(s_acc, 1)

                    masks(0)
                    for g in range(n_groups):
                        if g + 1 < n_groups:
                            masks(g + 1)
                        dve.wait_ge(s_exp, g + 1)
                        dve.wait_ge(s_mask, g + 1)
                        if g >= N_WT:
                            dve.wait_ge(s_sum, g - N_WT + 1)
                        both = mask[:, g % N_EXP, :, :].rearrange("p h w -> p (h w)")
                        dve.scalar_tensor_tensor(wt[:, g % N_WT, :, :], expo[:, g % N_EXP, :, :], 1.0,
                                                 both.unsqueeze(1).to_broadcast([P, HEADS + 1, TILES * WIN]),
                                                 ALU.max, ALU.min).then_inc(s_wt, 1)
                        if g >= 1:
                            add_sums(g - 1)
                        dve.wait_ge(s_wt, g + 1)
                        dve.tensor_reduce(
                            a_sum[:, g % N_WT, :, 0:HEADS].rearrange("p h k -> p k h"),
                            wt[:, g % N_WT, 0:HEADS, :].rearrange("p k (h w) -> p k h w", h=TILES),
                            AX, ALU.add).then_inc(s_as, 1)
                    add_sums(n_groups - 1)

            nc.all_engine_barrier(sems_to_clear=range(s_first.num, s_last.num + 1))
            nc.regs_load(more_reg, more[0:1, 0:1])
            nc.br_cmp(more_reg, 0, on_true="pass_end", on_false="pass_start", comp_op="IS_EQ",
                      engines=mybir.ALL_ENGINES)
        nc.switch_bb("pass_end")

        hidden, at = area(0, 2, COLS)
        y, at = area(at, 3, CHUNK, P)
        res, at = area(at, 3, CHUNK, P)
        stats, at = area(at, 2, CHUNK, 6)
        moments, at = area(at, 2, CHUNK, 2)
        deviation, at = area(at, 2, CHUNK)
        assert at <= WORK

        s_at = sem("s_at")
        s_d3 = sem("s_d3")
        s_pt3 = sem("s_pt3")
        s_pc3 = sem("s_pc3")
        s_bs = sem("s_bs")
        s_sc = sem("s_sc")
        s_01 = sem("s_01")
        s_u1 = sem("s_u1")
        s_hid = sem("s_hid")
        s_u2 = sem("s_u2")
        s_y = sem("s_y")
        s_chain = sem("s_chain")
        s_var = sem("s_var")
        s_dev = sem("s_dev")
        s_res = sem("s_res")
        s_out = [sem(f"s_out{j}") for j in range(3)]

        with nc.Block() as block:
            @block.tensor
            def _(pe):
                for i in range(n_blocks):
                    last = pe.transpose(bank[7][:, i * 4:(i + 1) * 4], acc[0:4, HEADS, i * P:(i + 1) * P],
                                        ident[0:4, 0:4])
                last.then_inc(s_at, 1)
                s_pt_now[0] = s_pt3
                transpose_parts(pe, (s_d3, 8))
                pe.wait_ge(s_pc3, n_part_banks)

                def broadcast(c):
                    if c >= 1:
                        pe.wait_ge(s_sc, c)
                    n = nodes_of(c)
                    for k in range(HEADS):
                        last = pe.matmul(bank[k][:, 0:n], pick[:, k, :], split[:, c * COLS:c * COLS + n],
                                         start=True, stop=True)
                    last.then_inc(s_bs, 1)

                def second(c):
                    pe.wait_ge(s_hid, c + 1)
                    if c >= 2:
                        pe.wait_ge(s_y, c - 1)
                    for i in range(blocks_of(c)):
                        m = block_nodes(c * CHUNK + i)
                        last = pe.matmul(bank[5 + c % 2][0:m, i * P:(i + 1) * P],
                                         hidden[:, c % 2, i * P:i * P + m], wc2[:, :], start=True, stop=True)
                    last.then_inc(s_u2, 1)

                broadcast(0)
                for c in range(n_chunks):
                    n = nodes_of(c)
                    cols = slice(c * COLS, c * COLS + n)
                    if c >= 2:
                        pe.wait_ge(s_hid, c - 1)
                    pe.matmul(bank[3 + c % 2][:, 0:n], wc1[:, 0, :], x_t[:, cols], start=True, stop=False)
                    if c + 1 < n_chunks:
                        broadcast(c + 1)
                    pe.wait_ge(s_sc, c + 1)
                    pe.matmul(bank[3 + c % 2][:, 0:n], wc1[:, 1, :], acc[:, 2, cols], start=False, stop=False)
                    pe.wait_ge(s_01, c + 1)
                    pe.matmul(bank[3 + c % 2][:, 0:n], wc1[:, 1, :], acc[:, 0, cols],
                              start=False, stop=True).then_inc(s_u1, 1)
                    if c >= 1:
                        second(c - 1)
                second(n_chunks - 1)

            @block.gpsimd
            def _(pool):
                for c in range(n_chunks):
                    cols = slice(c * COLS, c * COLS + nodes_of(c))
                    pool.wait_ge(s_sc, c + 1)
                    pool.tensor_tensor(acc[:, 0, cols], acc[:, 0, cols], acc[:, 1, cols],
                                       ALU.add).then_inc(s_01, 1)

            @block.scalar
            def _(act):
                s_pt_now[0] = s_pt3
                copy_parts(act, s_pc3)

                def deviations(c):
                    m, nb = min(nodes_of(c), P), blocks_of(c)
                    act.wait_ge(s_var, c + 1)
                    act.activation(deviation[0:m, c % 2, 0:nb], moments[0:m, c % 2, 0:nb, 1], ACT.Sqrt,
                                   bias=eps_col[0:m, 0:1]).then_inc(s_dev, 1)

                for c in range(n_chunks):
                    n = nodes_of(c)
                    act.wait_ge(s_u1, c + 1)
                    if c >= 2:
                        act.wait_ge(s_u2, c - 1)
                    act.activation(hidden[:, c % 2, 0:n], bank[3 + c % 2][:, 0:n], ACT.Relu,
                                   bias=bc1[:, 0:1]).then_inc(s_hid, 1)
                    if c >= 1:
                        deviations(c - 1)
                deviations(n_chunks - 1)

            @block.vector
            def _(dve):
                chain = chained(dve, s_d3)
                dve.wait_ge(s_at, 1)
                chain(dve.tensor_scalar_max(per_node[:, :, :],
                                            bank[7][:, 0:n_blocks * 4].rearrange("p (i j) -> p i j", j=4), 1.0))
                chain(dve.reciprocal(per_node[:, :, :], per_node[:, :, :]))
                chain(dve.scalar_tensor_tensor(
                    per_node[:, :, 0:HEADS], per_node[:, :, 0:HEADS], 1.0 / HEADS,
                    per_node[:, :, HEADS:HEADS + 1].to_broadcast([P, n_blocks, HEADS]), ALU.mult, ALU.mult))
                split_parts(dve, chain)
                chain = chained(dve, s_chain)

                def scale(c):
                    cols = slice(c * COLS, c * COLS + nodes_of(c))
                    dve.wait_ge(s_bs, c + 1)
                    for k in range(HEADS):
                        last = dve.tensor_tensor(acc[:, k, cols], acc[:, k, cols],
                                                 bank[k][:, 0:nodes_of(c)], ALU.mult)
                    last.then_inc(s_sc, 1)

                def moments_of(c):
                    m, nb = min(nodes_of(c), P), blocks_of(c)
                    dve.wait_ge(s_u2, c + 1)
                    if c >= 3:
                        dve.wait_ge(s_res, c - 2)
                    dve.tensor_tensor(y[0:m, c % 3, 0:nb, :],
                                      bank[5 + c % 2][0:m, 0:nb * P].rearrange("p (i f) -> p i f", f=P),
                                      x_rows[0:m, c * CHUNK:c * CHUNK + nb, :], ALU.add).then_inc(s_y, 1)
                    dve.wait_ge(s_y, c + 1)
                    for i in range(nb):
                        last = dve.bn_stats(stats[0:m, c % 2, i, :], y[0:m, c % 3, i, :])
                    chain(last)
                    for i in range(nb):
                        last = dve.bn_aggr(moments[0:m, c % 2, i, :], stats[0:m, c % 2, i, :])
                    last.then_inc(s_var, 1)

                def normalise(c):
                    m, nb = min(nodes_of(c), P), blocks_of(c)
                    dve.wait_ge(s_dev, c + 1)
                    chain(dve.reciprocal(deviation[0:m, c % 2, 0:nb], deviation[0:m, c % 2, 0:nb]))
                    if c >= 3:
                        dve.wait_ge(s_out[c % 3], 16 * (c // 3))
                    for i in range(nb):
                        last = dve.tensor_scalar(res[0:m, c % 3, i, :], y[0:m, c % 3, i, :],
                                                 moments[0:m, c % 2, i, 0:1], deviation[0:m, c % 2, i:i + 1],
                                                 ALU.subtract, ALU.mult)
                    last.then_inc(s_res, 1)

                scale(0)
                for c in range(n_chunks + 2):
                    if c + 1 < n_chunks:
                        scale(c + 1)
                    if 0 <= c - 1 < n_chunks:
                        moments_of(c - 1)
                    if 0 <= c - 2 < n_chunks:
                        normalise(c - 2)

            @block.sync
            def _(sp):
                for c in range(n_chunks):
                    n = nodes_of(c)
                    sp.wait_ge(s_res, c + 1)
                    if n == COLS:
                        to = out[c * COLS:(c + 1) * COLS, :].rearrange("(i p) f -> p i f", p=P)
                        of = res[:, c % 3, :, :]
                    else:
                        to, of = out[c * COLS:n_nodes, :], res[0:n, c % 3, 0, :]
                    sp.dma_start(to, of).then_inc(s_out[c % 3], 16)
                for j in range(3):
                    sp.wait_ge(s_out[j], 16 * len(range(j, n_chunks, 3)))


_INS = ["x", "src", "dst",
        "L0_gnn_W_msg_1", "L0_gnn_W_msg_2", "L0_gnn_W_msg_3", "L0_gnn_b_msg_1", "L0_gnn_b_msg_2", "L0_gnn_b_msg_3",
        "L0_gnn_W_att_1", "L0_gnn_W_att_2", "L0_gnn_W_att_3", "L0_gnn_b_att_1", "L0_gnn_b_att_2", "L0_gnn_b_att_3",
        "L0_gnn_W_c1", "L0_gnn_b_c1", "L0_gnn_W_c2", "L0_gnn_b_c2"]


def kernel(**inputs):
    import numpy as np
    import concourse.bacc as bacc
    from concourse.bass_utils import run_bass_kernel_spmd

    nc = bacc.Bacc("TRN2", target_bir_lowering=False, num_devices=1)
    arrays, a = {}, {}
    for name in _INS:
        v = np.ascontiguousarray(inputs[name])
        arrays[f"in_{name}"] = v
        a[name.replace("L0_gnn_", "")] = nc.dram_tensor(
            f"in_{name}", v.shape, mybir.dt.from_np(v.dtype), kind="ExternalInput").ap()
    n, d = inputs["x"].shape
    table = nc.dram_tensor("message_table", (n, ROW), mybir.dt.float32, kind="Internal").ap()
    out = nc.dram_tensor("out", (n, d), mybir.dt.float32, kind="ExternalOutput").ap()
    gnn_program(nc, a["x"], a["src"], a["dst"], [a[f"W_msg_{k}"] for k in (1, 2, 3)],
                [a[f"b_msg_{k}"] for k in (1, 2, 3)], [a[f"W_att_{k}"] for k in (1, 2, 3)],
                [a[f"b_att_{k}"] for k in (1, 2, 3)], a["W_c1"], a["b_c1"], a["W_c2"], a["b_c2"], table, out)
    r = run_bass_kernel_spmd(nc, [arrays], core_ids=[0])
    return r.results[0]["out"]
```

```python
import concourse.bass as bass
import concourse.mybir as mybir
from contextlib import ExitStack

P = 128
HEADS = 3
WIN = 48
TILES = 2
GROUP = TILES * P
ROW = P + HEADS
CHUNK = 4
COLS = CHUNK * P
DONE = float(1 << 20)
FLT_MAX = 3.4028234663852886e38
EPS = 1e-5

EARLY = 14
RING = 6
N_EXP = 3
N_WT = 3
N_SUM = 3
N_QW = 2
REGS = 16
STEP = 2


def gnn_program(nc, x, src, dst, w_msg, b_msg, w_att, b_att, w_c1, b_c1, w_c2, b_c2, table, out):
    f32, bf16, i32 = mybir.dt.float32, mybir.dt.bfloat16, mybir.dt.int32
    ALU, ACT, AX = mybir.AluOpType, mybir.ActivationFunctionType, mybir.AxisListType.X

    n_nodes = x.shape[0]
    n_edges = src.shape[0]
    n_blocks = -(-n_nodes // P)
    n_cols = n_blocks * P
    n_pad = -(-max(n_cols, n_nodes + WIN) // 32) * 32
    n_chunks = -(-n_blocks // CHUNK)
    n_groups = -(-n_edges // GROUP)
    n_rows = -(-n_groups // P)
    full_groups = n_edges // GROUP
    tail_edges = n_edges - full_groups * GROUP
    pair = CHUNK // TILES
    n_early = EARLY * pair
    assert n_early <= min(P, full_groups)

    def blocks_of(c):
        return min(CHUNK, n_blocks - c * CHUNK)

    def nodes_of(c):
        return min(COLS, n_nodes - c * COLS)

    def block_nodes(i):
        return min(P, n_nodes - i * P)

    def tile_edges(g, h):
        return min(P, n_edges - g * GROUP - h * P)

    ctx = ExitStack()
    with ctx:
        def sb(name, shape, dt=f32):
            return ctx.enter_context(nc.sbuf_tensor(name, shape, dt))

        def sem(name):
            return ctx.enter_context(nc.semaphore(name))

        early = sb("early", [P, EARLY * CHUNK, ROW])
        assert n_chunks <= EARLY
        x_rows = early[:, :, :].rearrange("p t r -> p (t r)")[:, 0:n_blocks * P].rearrange(
            "p (i f) -> p i f", f=P)
        x_t = sb("x_t", [P, n_cols])
        acc = sb("acc", [P, HEADS + 1, n_pad])
        split = sb("split", [3 * HEADS, n_pad], bf16)
        w1 = sb("w1", [P, P])
        w2 = sb("w2", [P, P])
        w3 = sb("w3", [P, P])
        wc1 = sb("wc1", [P, 2, P])
        wc2 = sb("wc2", [P, P])
        w_logit = sb("w_logit", [P, 2 * HEADS])
        b1 = sb("b1", [P, 1])
        b2 = sb("b2", [P, 1])
        bc1 = sb("bc1", [P, 1])
        b3_all = sb("b3_all", [P, P])
        bc2_all = sb("bc2_all", [P, P])
        b_logit = sb("b_logit", [P, HEADS])
        ident = sb("ident", [P, P])
        ident_bf = sb("ident_bf", [P, P], bf16)
        pick = sb("pick", [3 * HEADS, HEADS, P], bf16)
        columns = sb("columns", [P, WIN])
        columns_i = sb("columns_i", [P, WIN], i32)
        per_node = sb("per_node", [P, n_blocks, 4])
        part_rest = sb("part_rest", [P, n_blocks, HEADS])
        parts = sb("parts", [P, n_blocks, 3 * HEADS], bf16)
        eps_col = sb("eps_col", [P, 1])
        wc2_sum = sb("wc2_sum", [P, 1])
        x_sum = sb("x_sum", [P, CHUNK])

        n_ids = 2 * n_rows * GROUP
        ids_i = acc[:, HEADS, 0:n_ids].bitcast(i32).rearrange("p (j r e) -> p j r e", j=2, e=GROUP)
        dst_left = sb("dst_left", [P, n_rows, GROUP])
        src_t = sb("src_t", [P, TILES, n_rows * P], i32)
        dst_t = sb("dst_t", [P, TILES, n_rows * P])
        win_row = sb("win_row", [1, n_rows * P], i32)
        win_col = sb("win_col", [P, n_rows])
        least = sb("least", [P, 1])
        least_all = sb("least_all", [1, 1])
        more = sb("more", [1, 1], i32)

        WORK = 5250
        work = sb("work", [P, WORK])

        def area(at, *dims):
            n = 1
            for d in dims:
                n *= d
            view = work[:, at:at + n]
            if len(dims) == 2:
                view = view.rearrange("p (a b) -> p a b", a=dims[0])
            if len(dims) == 3:
                view = view.rearrange("p (a b c) -> p a b c", a=dims[0], b=dims[1])
            if len(dims) == 4:
                view = view.rearrange("p (a b c d) -> p a b c d", a=dims[0], b=dims[1], c=dims[2])
            return view, at + n

        bank = [ctx.enter_context(nc.psum_tensor(f"bank{i}", [P, 512], f32)) for i in range(8)]

        def bank_bf(i):
            return bank[i][:, :].bitcast(bf16)

        h1, at = area(0, 2, COLS)
        h2, at = area(at, 2, COLS)
        src_f, _ = area(at, n_rows, GROUP)
        rows, at = area(at, 2, CHUNK, ROW)
        assert n_rows * GROUP <= 2 * CHUNK * ROW
        X_RING = 4
        x_in, at = area(at, X_RING, CHUNK, P)
        assert at <= WORK

        T_BANK, L1_BANK, L2_BANK, L3_BANK, LOGIT_BANK, PARTS_BANK = 0, 2, 3, 4, 6, 7
        IDS_BANKS = (1, PARTS_BANK)
        n_id_dmas = (full_groups // P + (full_groups % P > 0) + (tail_edges > 0))

        s_wb = [sem(f"s_wb{j}") for j in range(3)]
        s_wl = sem("s_wl")
        s_wu = sem("s_wu")
        s_x = [sem(f"s_x{c}") for c in range(n_chunks)]
        s_ids = [sem("s_src_in"), sem("s_dst_in")]
        s_idz = sem("s_idz")
        s_const = sem("s_const")
        s_cdve = sem("s_cdve")
        s_tr = sem("s_tr")
        s_xt = sem("s_xt")
        s_l1 = sem("s_l1")
        s_h1 = sem("s_h1")
        s_l2 = sem("s_l2")
        s_h2 = sem("s_h2")
        s_l3 = sem("s_l3")
        s_msg = sem("s_msg")
        s_pq = sem("s_pq")
        s_row = sem("s_row")
        s_tab = [sem(f"s_tab{j}") for j in range(2)]
        s_split = sem("s_split")
        s_pt = sem("s_pt")
        s_pc = sem("s_pc")
        s_srcf = sem("s_srcf")
        s_srct = sem("s_srct")
        s_src = sem("s_src")
        s_dst = sem("s_dst")
        s_cen = sem("s_cen")
        s_early = sem("s_early")
        SPLIT_STEPS = 5

        def split_parts(dve, chain, blocks):
            value = per_node[:, blocks, 0:HEADS]
            for j in range(3):
                part = parts[:, blocks, j * HEADS:(j + 1) * HEADS]
                chain(dve.tensor_copy(part, value))
                if j < 2:
                    chain(dve.tensor_tensor(part_rest[:, blocks, :], value, part, ALU.subtract))
                    value = part_rest[:, blocks, :]

        def transpose_parts(pe, to, blocks):
            for i in blocks:
                at = (i - blocks[0]) * P
                last = pe.transpose(to[0:3 * HEADS, at:at + P], parts[:, i, :], ident_bf[:, :])
            return last

        def chained(eng, s):
            count = [0]

            def chain(instruction):
                count[0] += 1
                instruction.then_inc(s, 1)
                eng.wait_ge(s, count[0])
                return count[0]
            return chain

        def column(v):
            return v.rearrange("(p o) -> p o", o=1)

        with nc.Block() as block:
            @block.sync
            def _(sp):
                def load_ids(j, ids):
                    done = 0
                    for r in range(full_groups // P):
                        if r == n_rows - 1:
                            sp.wait_ge(s_idz, 2)
                        sp.dma_start(ids_i[:, j, r, :],
                                     ids[r * P * GROUP:(r + 1) * P * GROUP].rearrange("(p e) -> p e", e=GROUP)
                                     ).then_inc(s_ids[j], 16)
                        done = (r + 1) * P
                    left = full_groups - done
                    sp.wait_ge(s_idz, 2)
                    if left:
                        sp.dma_start(ids_i[0:left, j, done // P, :],
                                     ids[done * GROUP:full_groups * GROUP].rearrange("(p e) -> p e", e=GROUP)
                                     ).then_inc(s_ids[j], 16)
                    if tail_edges:
                        p, r = full_groups % P, full_groups // P
                        sp.dma_start(ids_i[p:p + 1, j, r, 0:tail_edges],
                                     ids[full_groups * GROUP:n_edges].rearrange("(p e) -> p e", p=1)
                                     ).then_inc(s_ids[j], 16)

                def load_x(c):
                    n = nodes_of(c)
                    if c >= X_RING:
                        sp.wait_ge(s_tr, c - X_RING + 1)
                    if n == COLS:
                        to = x_in[:, c % X_RING, :, :]
                        of = x[c * COLS:(c + 1) * COLS, :].rearrange("(i p) f -> p i f", p=P)
                    else:
                        assert n <= P
                        to, of = x_in[0:n, c % X_RING, 0, :], x[c * COLS:n_nodes, :]
                    sp.dma_start(to, of).then_inc(s_x[c], 16)

                def store_rows(c):
                    n = nodes_of(c)
                    sp.wait_ge(s_row, c + 1)
                    if n == COLS:
                        to = table[c * COLS:(c + 1) * COLS, :].rearrange("(i p) f -> p i f", p=P)
                        of = rows[:, c % 2, :, :]
                    else:
                        to, of = table[c * COLS:n_nodes, :], rows[0:n, c % 2, 0, :]
                    sp.dma_start(to, of).then_inc(s_tab[c % 2], 16)

                load_ids(0, src)
                AHEAD = 7
                for c in range(n_chunks + AHEAD):
                    if c < n_chunks:
                        load_x(c)
                    if c == X_RING - 1:
                        load_ids(1, dst)
                        for to, of in ((bc1[:, :], column(b_c1)), (bc2_all[:, :], b_c2.partition_broadcast(P)),
                                       (wc1[:, :, :], w_c1.rearrange("(h p) f -> p h f", p=P)),
                                       (wc2[:, :], w_c2)):
                            sp.dma_start(to, of).then_inc(s_wu, 16)
                    if c >= AHEAD:
                        store_rows(c - AHEAD)
                for j in range(2):
                    sp.wait_ge(s_tab[j], 16 * len(range(j, n_chunks, 2)))

            @block.scalar
            def _(act):
                for to, of, s in ((w1, w_msg[0], s_wb[0]), (b1, column(b_msg[0]), s_wb[0]),
                                  (w2, w_msg[1], s_wb[1]), (b2, column(b_msg[1]), s_wb[1]),
                                  (w3, w_msg[2], s_wb[2]), (b3_all, b_msg[2].partition_broadcast(P), s_wb[2])):
                    act.dma_start(to[:, :], of).then_inc(s, 16)
                for k in range(HEADS):
                    for h in range(2):
                        act.dma_start(w_logit[:, h * HEADS + k:h * HEADS + k + 1],
                                      w_att[k][h * P:(h + 1) * P, :]).then_inc(s_wl, 16)
                    act.dma_start(b_logit[:, k:k + 1], b_att[k].partition_broadcast(P)).then_inc(s_wl, 16)
                act.wait_ge(s_wb[0], 32)
                for c in range(n_chunks + 5):
                    if c < n_chunks:
                        n = nodes_of(c)
                        act.wait_ge(s_tr, c + 1)
                        act.copy(x_t[:, c * COLS:c * COLS + n], bank[T_BANK][:, 0:n]).then_inc(s_xt, 1)
                    if 1 <= c <= n_chunks:
                        n = nodes_of(c - 1)
                        act.wait_ge(s_l1, c)
                        if c >= 3:
                            act.wait_ge(s_l2, c - 2)
                        act.activation(h1[:, (c - 1) % 2, 0:n], bank[L1_BANK][:, 0:n], ACT.Relu,
                                       bias=b1[:, 0:1]).then_inc(s_h1, 1)
                    if 0 <= c - 4 < n_chunks:
                        d, nb, m = c - 4, blocks_of(c - 4), min(nodes_of(c - 4), P)
                        act.wait_ge(s_msg, d + 1)
                        act.activation(rows[0:m, d % 2, 0:nb, 0:P], rows[0:m, d % 2, 0:nb, 0:P],
                                       ACT.Relu).then_inc(s_row, 1)
                    if c >= 5:
                        d, n = c - 5, blocks_of(c - 5) * P
                        act.wait_ge(s_pt, d + 1)
                        act.copy(split[:, d * COLS:d * COLS + n],
                                 bank_bf(PARTS_BANK)[0:3 * HEADS, 0:n]).then_inc(s_pc, 1)

            @block.vector
            def _(dve):
                for j in range(2):
                    dve.memset(ids_i[:, j, n_rows - 1, :], int(DONE) * j).then_inc(s_idz, 1)
                chain = chained(dve, s_cdve)
                dve.memset(eps_col[:, :], EPS)
                dve.memset(split[:, n_cols:n_pad], 0.0)
                dve.memset(x_t[:, n_nodes:n_cols], 0.0)
                chain(dve.memset(per_node[:, :, :], 0.0))
                dve.wait_ge(s_ids[0], 16 * n_id_dmas)
                dve.tensor_copy(src_f, ids_i[:, 0, :, :]).then_inc(s_srcf, 1)
                dve.wait_ge(s_const, 6)
                chain(dve.tensor_copy(ident_bf[:, :], ident[:, :]))
                chain(dve.tensor_copy(columns[:, :], columns_i[:, :]))
                for h in range(TILES):
                    dve.wait_ge(s_srct, h + 1)
                    dve.tensor_copy(src_t[:, h, :], bank[IDS_BANKS[h]][:, 0:n_rows * P]).then_inc(s_src, 1)
                acc_flat = acc[:, :, :].rearrange("p k n -> p (k n)")
                ids_at, zeros = HEADS * n_pad, 4 * n_pad
                share = -(-(zeros - n_ids) // n_chunks)

                def zero(a, b):
                    if b > a:
                        dve.memset(acc_flat[:, a:b], 0.0)

                dve.wait_ge(s_wb[1], 32)
                split_chain = chained(dve, s_split)
                for c in range(n_chunks + 1):
                    if c < n_chunks:
                        n = nodes_of(c)
                        dve.wait_ge(s_l2, c + 1)
                        if c >= 2:
                            dve.wait_ge(s_l3, c - 1)
                        dve.tensor_scalar(h2[:, c % 2, 0:n], bank[L2_BANK][:, 0:n], b2[:, 0:1], 0.0,
                                          ALU.add, ALU.max).then_inc(s_h2, 1)
                    if c == 0:
                        dve.wait_ge(s_wb[2], 32)
                        dve.wait_ge(s_wl, 16 * 3 * HEADS)
                    if c >= 1:
                        d = c - 1
                        nb, m = blocks_of(d), min(nodes_of(d), P)
                        mine = slice(d * CHUNK, d * CHUNK + nb)
                        dve.wait_ge(s_l3, d + 1)
                        if d >= 2:
                            dve.wait_ge(s_tab[d % 2], 16 * (d // 2))
                        logits = bank[LOGIT_BANK][0:m, 0:nb * 6].rearrange("p (i j) -> p i j", j=6)
                        dve.tensor_copy(rows[0:m, d % 2, 0:nb, P:ROW], logits[:, :, 0:HEADS])
                        dve.tensor_tensor(per_node[0:m, mine, 0:HEADS], logits[:, :, HEADS:2 * HEADS],
                                          b_logit[0:m, :].unsqueeze(1).to_broadcast([m, nb, HEADS]),
                                          ALU.add).then_inc(s_pq, 1)
                        dve.tensor_tensor(rows[0:m, d % 2, 0:nb, 0:P],
                                          bank[L3_BANK + d % 2][0:m, 0:nb * P].rearrange(
                                              "p (i f) -> p i f", f=P),
                                          b3_all[0:m, :].unsqueeze(1).to_broadcast([m, nb, P]),
                                          ALU.add).then_inc(s_msg, 1)
                        dve.wait_ge(s_pq, d + 1)
                        split_parts(dve, split_chain, mine)
                    if c == 2:
                        dve.wait_ge(s_ids[1], 16 * n_id_dmas)
                        dve.tensor_copy(dst_left[:, :, :], ids_i[:, 1, :, :]).then_inc(s_dst, 1)
                    if c == 3:
                        dve.wait_ge(s_wu, 64)
                        centre = chained(dve, s_cen)
                        centre(dve.tensor_reduce(wc2_sum[:, :], wc2[:, :], AX, ALU.add))
                        centre(dve.scalar_tensor_tensor(wc2[:, :], wc2_sum[:, 0:1].to_broadcast([P, P]), -1.0 / P,
                                                        wc2[:, :], ALU.mult, ALU.add))
                    if c < n_chunks:
                        a, b = c * share, min((c + 1) * share, zeros - n_ids)
                        zero(a, min(b, ids_at))
                        zero(max(a, ids_at) + n_ids, b + n_ids)
                    else:
                        dve.wait_ge(s_dst, 1)
                        zero(ids_at, ids_at + n_ids)

            @block.gpsimd
            def _(pool):
                pool.memset(ident[:, :], 0.0).then_inc(s_const, 1)
                pool.memset(pick[:, :, :], 0.0).then_inc(s_const, 1)
                pool.iota(columns_i[:, :], pattern=[[1, WIN]], base=0,
                          channel_multiplier=0).then_inc(s_const, 1)
                pool.wait_ge(s_const, 3)
                pool.affine_select(out=ident[:, :], in_=ident[:, :], compare_op=ALU.not_equal, fill=1.0,
                                   base=0, pattern=[[-1, P]], channel_multiplier=1).then_inc(s_const, 1)
                for part in range(3):
                    pool.affine_select(out=pick[:, :, :], in_=pick[:, :, :], compare_op=ALU.not_equal,
                                       fill=1.0, base=-HEADS * part, pattern=[[-1, HEADS], [0, P]],
                                       channel_multiplier=1).then_inc(s_const, 1)
                    pool.wait_ge(s_const, 5 + part)
                pool.wait_ge(s_src, TILES)
                for t in range(EARLY * CHUNK):
                    g, h = t // TILES, t % TILES
                    pool.indirect_dma_start(
                        out=early[:, t, 0:P], out_offset=None, in_=x[:, :],
                        in_offset=bass.IndirectOffsetOnAxis(ap=src_t[:, h, g:g + 1], axis=0),
                    ).then_inc(s_early, 16)

            @block.tensor
            def _(pe):
                pe.wait_ge(s_const, 4)
                pe.wait_ge(s_srcf, 1)
                for h in range(TILES):
                    for r in range(n_rows):
                        last = pe.transpose(bank[IDS_BANKS[h]][:, r * P:(r + 1) * P],
                                            src_f[:, r, h * P:(h + 1) * P], ident[:, :])
                    last.then_inc(s_srct, 1)
                for s in range(n_chunks + 5):
                    if s < n_chunks:
                        c = s
                        pe.wait_ge(s_x[c], 16)
                        if c >= 1:
                            pe.wait_ge(s_xt, c)
                        for i in range(blocks_of(c)):
                            m = block_nodes(c * CHUNK + i)
                            last = pe.transpose(bank[T_BANK][:, i * P:i * P + m],
                                                x_in[0:m, c % X_RING, i, :], ident[0:m, 0:m])
                        last.then_inc(s_tr, 1)
                    if 0 <= s - 1 < n_chunks:
                        c, n = s - 1, nodes_of(s - 1)
                        if c == 0:
                            pe.wait_ge(s_wb[0], 32)
                        pe.wait_ge(s_xt, c + 1)
                        if c >= 1:
                            pe.wait_ge(s_h1, c)
                        pe.matmul(bank[L1_BANK][:, 0:n], w1[:, :], x_t[:, c * COLS:c * COLS + n],
                                  start=True, stop=True).then_inc(s_l1, 1)
                    if 0 <= s - 2 < n_chunks:
                        c, n = s - 2, nodes_of(s - 2)
                        if c == 0:
                            pe.wait_ge(s_wb[1], 32)
                        pe.wait_ge(s_h1, c + 1)
                        if c >= 1:
                            pe.wait_ge(s_h2, c)
                        pe.matmul(bank[L2_BANK][:, 0:n], w2[:, :], h1[:, c % 2, 0:n],
                                  start=True, stop=True).then_inc(s_l2, 1)
                    if 0 <= s - 5 < n_chunks:
                        c = s - 5
                        if c == 0:
                            pe.wait_ge(s_cdve, 2)
                        pe.wait_ge(s_split, SPLIT_STEPS * (c + 1))
                        if c >= 1:
                            pe.wait_ge(s_pc, c)
                        transpose_parts(pe, bank_bf(PARTS_BANK),
                                        range(c * CHUNK, c * CHUNK + blocks_of(c))).then_inc(s_pt, 1)
                    if 0 <= s - 3 < n_chunks:
                        c = s - 3
                        if c == 0:
                            pe.wait_ge(s_wb[2], 32)
                            pe.wait_ge(s_wl, 16 * 3 * HEADS)
                        pe.wait_ge(s_h2, c + 1)
                        if c >= 1:
                            pe.wait_ge(s_pq, c)
                        if c >= 2:
                            pe.wait_ge(s_msg, c - 1)
                        for i in range(blocks_of(c)):
                            b = c * CHUNK + i
                            m = block_nodes(b)
                            pe.matmul(bank[L3_BANK + c % 2][0:m, i * P:(i + 1) * P],
                                      h2[:, c % 2, i * P:i * P + m], w3[:, :], start=True, stop=True)
                            last = pe.matmul(bank[LOGIT_BANK][0:m, i * 6:(i + 1) * 6],
                                             x_t[:, b * P:b * P + m], w_logit[:, :], start=True, stop=True)
                        last.then_inc(s_l3, 1)

        nc.all_engine_barrier()

        gath, at = area(0, RING * TILES, ROW)
        dist, at2 = area(at, n_rows, GROUP)
        hit, at2 = area(at2, n_rows, GROUP)
        assert at2 <= WORK
        expo, at = area(at, N_EXP, HEADS + 1, TILES * WIN)
        mask, at = area(at, N_EXP, TILES, WIN)
        wt, at = area(at, N_WT, HEADS + 1, TILES * WIN)
        a_sum, at = area(at, N_WT, TILES, HEADS + 1)
        early_x, at = area(at, 1, COLS)
        early_h, at = area(at, 1, COLS)
        assert at <= WORK

        EARLY_BANKS = (5, 6, 7)

        EARLY_STAGES = 6
        between = (n_groups - n_early) // EARLY
        lead = STEP * EARLY_STAGES
        assert between >= lead
        first_order = []
        starts = {}
        for e in range(EARLY):
            others = range(n_early + e * between, n_early + (e + 1) * between)
            starts[e] = len(first_order)
            first_order += others[:lead]
            for g in range(e * pair, (e + 1) * pair):
                first_order.append(g)
            first_order += others[lead:]
        first_order += range(n_early + EARLY * between, n_groups)
        early_done = [first_order.index((e + 1) * pair - 1) for e in range(EARLY)]

        s_xr = [sem(f"s_xr{c}") for c in range(n_chunks)]
        s_first = sem("s_first")
        s_prep = sem("s_prep")
        s_ptr = sem("s_ptr")
        s_gath = [sem(f"s_gath{j}") for j in range(RING * TILES)]
        s_fill = sem("s_fill")
        s_qw = sem("s_qw")
        s_exp = sem("s_exp")
        s_mask = sem("s_mask")
        s_wt = sem("s_wt")
        s_as = sem("s_as")
        s_sum = sem("s_sum")
        s_acc = sem("s_acc")
        s_last = sem("s_last")

        def edge_pass(first):
            order = first_order if first else list(range(n_groups))
            n_own = n_early if first else 0
            others = [g for g in order if g >= n_own]
            turn = {g: n for n, g in enumerate(others)}
            position = {g: i for i, g in enumerate(order)}

            def rows_of(g, h):
                return early[:, g * TILES + h, :] if g < n_own else gath[:, (turn[g] % RING) * TILES + h, :]

            def rows_landed(eng, g, h):
                if g < n_own:
                    eng.wait_ge(s_row, n_chunks + g // pair + 1)
                else:
                    eng.wait_ge(s_gath[(turn[g] % RING) * TILES + h], 16 * (turn[g] // RING + 1))

            def stages(i):
                return [(e, (i - at) // STEP) for e, at in starts.items()
                        if first and i >= at and (i - at) % STEP == 0 and (i - at) // STEP < EARLY_STAGES]

            def window_registers(eng):
                regs = {}

                def window(g):
                    if g not in regs:
                        n = min(pair, n_own - g) if g < n_own else min(REGS, n_groups - g)
                        fresh = [eng.alloc_register(f"win{first}_{g + j}") for j in range(n)]
                        eng.load(fresh, win_row[0:1, g:g + n])
                        for j in range(n):
                            regs[g + j] = eng.snap(fresh[j], donate=True, min_val=0, max_val=n_nodes)
                    return regs.pop(g)
                return window

            with nc.Block() as block:
                @block.gpsimd
                def _(pool):
                    for n, g in enumerate(others):
                        if n >= RING:
                            pool.wait_ge(s_sum, position[others[n - RING]] + 1)
                        for h in range(TILES):
                            m = tile_edges(g, h)
                            slot = (n % RING) * TILES + h
                            pool.indirect_dma_start(
                                out=gath[0:m, slot, :], out_offset=None, in_=table[:, :],
                                in_offset=bass.IndirectOffsetOnAxis(ap=src_t[0:m, h, g:g + 1], axis=0),
                            ).then_inc(s_gath[slot], 16)
                    for j in range(RING * TILES):
                        pool.wait_ge(s_gath[j], 16 * len(range(j // TILES, len(others), RING)))

                if first:
                    @block.sync
                    def _(sp):
                        for c in range(n_chunks):
                            n = nodes_of(c)
                            sp.wait_ge(s_sum, early_done[c] + 1)
                            if n == COLS:
                                to = x_rows[:, c * CHUNK:(c + 1) * CHUNK, :]
                                of = x[c * COLS:(c + 1) * COLS, :].rearrange("(i p) f -> p i f", p=P)
                            else:
                                to, of = x_rows[0:n, c * CHUNK, :], x[c * COLS:n_nodes, :]
                            sp.dma_start(to, of).then_inc(s_xr[c], 16)

                @block.tensor
                def _(pe):
                    pe.wait_ge(s_prep, 3)
                    for h in range(TILES):
                        for r in range(n_rows):
                            last = pe.transpose(bank[h][:, r * P:(r + 1) * P],
                                                dist[:, r, h * P:(h + 1) * P], ident[:, :])
                    last.then_inc(s_ptr, 1)
                    for r in range(n_rows):
                        pe.transpose(bank[2][0:1, r * P:(r + 1) * P], win_col[:, r:r + 1], ident[:, :])
                    pe.wait_ge(s_prep, 6)
                    pe.transpose(bank[3][0:1, 0:P], least[:, :], ident[:, :]).then_inc(s_ptr, 1)
                    pe.wait_ge(s_prep, 9)
                    window = window_registers(pe)

                    def q_window(i):
                        start = window(order[i])
                        if i >= N_QW:
                            pe.wait_ge(s_exp, i - N_QW + 1)
                        for k in range(HEADS):
                            last = pe.matmul(bank[i % N_QW][:, k * WIN:(k + 1) * WIN], pick[:, k, :],
                                             split[:, bass.ds(start, WIN)], start=True, stop=True)
                        last.then_inc(s_qw, 1)

                    def early_stage(e, stage):
                        c = n_chunks + e
                        even, odd, logits = (bank[b] for b in EARLY_BANKS)
                        tiles = range(e * CHUNK, (e + 1) * CHUNK)
                        if stage == 0:
                            if e == 0:
                                pe.wait_ge(s_early, 16 * EARLY * CHUNK)
                            pe.wait_ge(s_h2, c)
                            for i, t in enumerate(tiles):
                                last = pe.transpose(even[:, i * P:(i + 1) * P], early[:, t, 0:P], ident[:, :])
                            last.then_inc(s_tr, 1)
                        elif stage == 1:
                            pe.wait_ge(s_xt, c + 1)
                            pe.wait_ge(s_msg, c)
                            pe.matmul(odd[:, :], w1[:, :], early_x[:, 0, :],
                                      start=True, stop=True).then_inc(s_l1, 1)
                        elif stage == 2:
                            pe.wait_ge(s_h1, c + 1)
                            pe.matmul(even[:, :], w2[:, :], early_h[:, 0, :],
                                      start=True, stop=True).then_inc(s_l2, 1)
                        elif stage == 3:
                            pe.wait_ge(s_h2, c + 1)
                            for i in range(CHUNK):
                                cols = slice(i * P, (i + 1) * P)
                                pe.matmul(odd[:, cols], early_h[:, 0, cols], w3[:, :], start=True, stop=True)
                                last = pe.matmul(logits[:, i * HEADS:(i + 1) * HEADS], early_x[:, 0, cols],
                                                 w_logit[:, 0:HEADS], start=True, stop=True)
                            last.then_inc(s_l3, 1)

                    for i in range(N_QW):
                        q_window(i)
                    pe.wait_ge(s_fill, 1)
                    for i, g in enumerate(order):
                        sums = bank[N_QW + i % N_SUM]
                        tiles = [h for h in range(TILES) if tile_edges(g, h) > 0]
                        pe.wait_ge(s_wt, i + 1)
                        if i >= N_SUM:
                            pe.wait_ge(s_acc, i - N_SUM + 1)
                        for h in tiles:
                            m = tile_edges(g, h)
                            rows_landed(pe, g, h)
                            pe.matmul(sums[:, 0:HEADS * WIN], rows_of(g, h)[0:m, 0:P],
                                      wt[0:m, i % N_WT, 0:HEADS, h * WIN:(h + 1) * WIN],
                                      start=h == tiles[0], stop=h == tiles[-1])
                        pe.wait_ge(s_as, i + 1)
                        for h in tiles:
                            m = tile_edges(g, h)
                            last = pe.matmul(sums[0:HEADS + 1, HEADS * WIN:(HEADS + 1) * WIN],
                                             a_sum[0:m, i % N_WT, h, :],
                                             wt[0:m, i % N_WT, HEADS, h * WIN:(h + 1) * WIN],
                                             start=h == tiles[0], stop=h == tiles[-1])
                        last.then_inc(s_sum, 1)
                        if i + N_QW < n_groups:
                            q_window(i + N_QW)
                        for e, stage in stages(i):
                            early_stage(e, stage)

                @block.scalar
                def _(act):
                    def early_stage(e, stage):
                        c = n_chunks + e
                        even, odd, _ = (bank[b] for b in EARLY_BANKS)
                        mine = slice(e * CHUNK, (e + 1) * CHUNK)
                        if stage == 1:
                            act.wait_ge(s_tr, c + 1)
                            act.wait_ge(s_l3, c)
                            act.copy(early_x[:, 0, :], even[:, :]).then_inc(s_xt, 1)
                        elif stage == 2:
                            act.wait_ge(s_l1, c + 1)
                            act.activation(early_h[:, 0, :], odd[:, :], ACT.Relu,
                                           bias=b1[:, 0:1]).then_inc(s_h1, 1)
                        elif stage == 5:
                            act.wait_ge(s_msg, c + 1)
                            act.activation(early[:, mine, 0:P], early[:, mine, 0:P], ACT.Relu).then_inc(s_row, 1)

                    for i, g in enumerate(order):
                        for e, stage in stages(i):
                            early_stage(e, stage)
                        act.wait_ge(s_qw, i + 1)
                        if i >= N_EXP:
                            act.wait_ge(s_wt, i - N_EXP + 1)
                        for h in range(TILES):
                            m = tile_edges(g, h)
                            rows_landed(act, g, h)
                            for k in range(HEADS):
                                last = act.activation(expo[0:m, i % N_EXP, k, h * WIN:(h + 1) * WIN],
                                                      bank[i % N_QW][0:m, k * WIN:(k + 1) * WIN], ACT.Exp,
                                                      bias=rows_of(g, h)[0:m, P + k:P + k + 1])
                        last.then_inc(s_exp, 1)

                @block.vector
                def _(dve):
                    chain = chained(dve, s_prep)
                    chain(dve.tensor_reduce(win_col[:, :], dst_left[:, :, :], AX, ALU.min))
                    chain(dve.tensor_scalar_min(win_col[:, :], win_col[:, :], float(n_nodes)))
                    chain(dve.tensor_tensor(dist[:, :, :], dst_left[:, :, :],
                                            win_col[:, :].unsqueeze(2).to_broadcast([P, n_rows, GROUP]),
                                            ALU.subtract))
                    chain(dve.tensor_scalar(hit[:, :, :], dist[:, :, :], float(WIN), DONE,
                                            ALU.is_lt, ALU.mult))
                    chain(dve.tensor_tensor(dst_left[:, :, :], dst_left[:, :, :], hit[:, :, :], ALU.add))
                    chain(dve.tensor_reduce(least[:, :], dst_left[:, :, :].rearrange("p r e -> p (r e)"),
                                            AX, ALU.min))
                    dve.wait_ge(s_ptr, 1)
                    for h in range(TILES):
                        dve.tensor_copy(dst_t[:, h, :], bank[h][:, 0:n_rows * P])
                    dve.wait_ge(s_ptr, 2)
                    chain(dve.tensor_copy(win_row[0:1, :], bank[2][0:1, 0:n_rows * P]))
                    chain(dve.tensor_reduce(least_all[:, :], bank[3][0:1, 0:P], AX, ALU.min))
                    chain(dve.tensor_scalar(more[:, :], least_all[:, :], DONE, None, ALU.is_lt))
                    for j in range(N_EXP):
                        dve.memset(expo[:, j, HEADS, :], 0.0)
                    dve.memset(a_sum[:, :, :, :], 1.0)
                    for j in range(N_SUM):
                        last = dve.memset(bank[N_QW + j][:, HEADS * WIN:(HEADS + 1) * WIN], 0.0)
                    last.then_inc(s_fill, 1)
                    dve.wait_ge(s_fill, 1)
                    window = window_registers(dve)

                    def masks(i):
                        g = order[i]
                        if i >= N_EXP:
                            dve.wait_ge(s_wt, i - N_EXP + 1)
                        for h in range(TILES):
                            last = dve.tensor_scalar(mask[:, i % N_EXP, h, :], columns[:, :],
                                                     dst_t[:, h, g:g + 1], FLT_MAX, ALU.is_equal, ALU.mult)
                        last.then_inc(s_mask, 1)

                    def add_sums(i):
                        start = window(order[i])
                        dve.wait_ge(s_sum, i + 1)
                        if i >= 1:
                            dve.wait_ge(s_acc, i)
                        here = acc[:, :, bass.ds(start, WIN)]
                        dve.tensor_tensor(here, here,
                                          bank[N_QW + i % N_SUM][:, 0:(HEADS + 1) * WIN].rearrange(
                                              "p (k w) -> p k w", w=WIN), ALU.add).then_inc(s_acc, 1)

                    def early_stage(e, stage):
                        c = n_chunks + e
                        even, odd, logits = (bank[b] for b in EARLY_BANKS)
                        mine = slice(e * CHUNK, (e + 1) * CHUNK)
                        if stage == 3:
                            dve.wait_ge(s_l2, c + 1)
                            dve.tensor_scalar(early_h[:, 0, :], even[:, :], b2[:, 0:1], 0.0,
                                              ALU.add, ALU.max).then_inc(s_h2, 1)
                        elif stage == 4:
                            dve.wait_ge(s_l3, c + 1)
                            dve.tensor_copy(early[:, mine, P:ROW], logits[:, 0:CHUNK * HEADS].rearrange(
                                "p (i k) -> p i k", k=HEADS))
                            dve.tensor_tensor(early[:, mine, 0:P],
                                              odd[:, :].rearrange("p (i f) -> p i f", f=P),
                                              b3_all[:, :].unsqueeze(1).to_broadcast([P, CHUNK, P]),
                                              ALU.add).then_inc(s_msg, 1)

                    def centre_x(c, step):
                        m, nb = min(nodes_of(c), P), blocks_of(c)
                        here = x_rows[0:m, c * CHUNK:c * CHUNK + nb, :]
                        dve.wait_ge(s_cen, 2 + 3 * c + step)
                        if step == 0:
                            dve.wait_ge(s_xr[c], 16)
                            last = dve.tensor_tensor(here, here, bc2_all[0:m, :].unsqueeze(1).to_broadcast(
                                [m, nb, P]), ALU.add)
                        elif step == 1:
                            last = dve.tensor_reduce(x_sum[0:m, 0:nb], here, AX, ALU.add)
                        else:
                            last = dve.scalar_tensor_tensor(
                                here, x_sum[0:m, 0:nb].unsqueeze(2).to_broadcast([m, nb, P]), -1.0 / P,
                                here, ALU.mult, ALU.add)
                        last.then_inc(s_cen, 1)

                    centre_at = {early_done[c] + STEP + 2 + step: (c, step)
                                 for c in range(n_chunks) for step in range(3)} if first else {}
                    masks(0)
                    for i, g in enumerate(order):
                        if i + 1 < n_groups:
                            masks(i + 1)
                        dve.wait_ge(s_exp, i + 1)
                        dve.wait_ge(s_mask, i + 1)
                        if i >= N_WT:
                            dve.wait_ge(s_sum, i - N_WT + 1)
                        both = mask[:, i % N_EXP, :, :].rearrange("p h w -> p (h w)")
                        dve.scalar_tensor_tensor(wt[:, i % N_WT, :, :], expo[:, i % N_EXP, :, :], 1.0,
                                                 both.unsqueeze(1).to_broadcast([P, HEADS + 1, TILES * WIN]),
                                                 ALU.max, ALU.min).then_inc(s_wt, 1)
                        if i >= 1:
                            add_sums(i - 1)
                        dve.wait_ge(s_wt, i + 1)
                        dve.tensor_reduce(
                            a_sum[:, i % N_WT, :, 0:HEADS].rearrange("p h k -> p k h"),
                            wt[:, i % N_WT, 0:HEADS, :].rearrange("p k (h w) -> p k h w", h=TILES),
                            AX, ALU.add).then_inc(s_as, 1)
                        for e, stage in stages(i):
                            early_stage(e, stage)
                        if i in centre_at:
                            centre_x(*centre_at[i])
                    add_sums(n_groups - 1)

        more_reg = nc.alloc_registers("more")

        def branch():
            nc.regs_load(more_reg, more[0:1, 0:1])
            nc.br_cmp(more_reg, 0, on_true="pass_end", on_false="pass_again", comp_op="IS_EQ",
                      engines=mybir.ALL_ENGINES)

        edge_pass(first=True)
        branch()
        with nc.body("pass_again", valid_engines=mybir.ALL_ENGINES):
            nc.gpsimd.dma_reset(range(s_first.num, s_last.num + 1))
            nc.all_engine_barrier(sems_to_clear=range(s_first.num, s_last.num + 1))
            edge_pass(first=False)
            branch()
        nc.switch_bb("pass_end")

        hidden, at = area(0, 2, COLS)
        y, at = area(at, 3, CHUNK, P)
        res, at = area(at, 3, CHUNK, P)
        square, at = area(at, CHUNK, P)
        spread, at = area(at, 3, CHUNK)
        deviation, at = area(at, 3, CHUNK)
        assert at <= WORK

        BANK_BLOCKS = 8
        SCALE_STEPS = 3 + SPLIT_STEPS
        stretches = [range(0, CHUNK), range(CHUNK, CHUNK + BANK_BLOCKS), range(CHUNK + BANK_BLOCKS, n_blocks)]
        loads = [(n, stretch[i:i + BANK_BLOCKS]) for n, stretch in enumerate(stretches)
                 for i in range(0, len(stretch), BANK_BLOCKS)]
        HEAD_BANKS, U1_BANKS, U2_BANKS = (0, 1, 2), (3, 4), (5, 6)
        SUMS_BANKS, LOAD_BANKS = (7, U1_BANKS[1], U1_BANKS[0]), U2_BANKS

        s_at = sem("s_at")
        s_d3 = sem("s_d3")
        s_pt3 = sem("s_pt3")
        s_pc3 = sem("s_pc3")
        s_bs = sem("s_bs")
        s_sc = sem("s_sc")
        s_hs = sem("s_hs")
        s_u1 = sem("s_u1")
        s_hid = sem("s_hid")
        s_u2 = sem("s_u2")
        s_y = sem("s_y")
        s_sq = sem("s_sq")
        s_dev = sem("s_dev")
        s_rec = sem("s_rec")
        s_res = sem("s_res")
        s_out = [sem(f"s_out{j}") for j in range(3)]

        def load_with(c):
            return next(b for b, (_, blocks) in enumerate(loads) if c * CHUNK + blocks_of(c) - 1 in blocks)

        with nc.Block() as block:
            @block.tensor
            def _(pe):
                def sums(n):
                    for i in stretches[n]:
                        last = pe.transpose(bank[SUMS_BANKS[n]][:, i * 4:(i + 1) * 4],
                                            acc[0:4, HEADS, i * P:(i + 1) * P], ident[0:4, 0:4])
                    last.then_inc(s_at, 1)

                def scales(b):
                    n, blocks = loads[b]
                    pe.wait_ge(s_d3, SCALE_STEPS * (n + 1))
                    if b >= 2:
                        pe.wait_ge(s_pc3, b - 1)
                    transpose_parts(pe, bank_bf(LOAD_BANKS[b % 2]), blocks).then_inc(s_pt3, 1)

                def broadcast(c):
                    if c >= 1:
                        pe.wait_ge(s_sc, c)
                    pe.wait_ge(s_pc3, load_with(c) + 1)
                    n = nodes_of(c)
                    for k in range(HEADS):
                        last = pe.matmul(bank[HEAD_BANKS[k]][:, 0:n], pick[:, k, :],
                                         split[:, c * COLS:c * COLS + n], start=True, stop=True)
                    last.then_inc(s_bs, 1)

                def first_of_x(c):
                    n = nodes_of(c)
                    if c < 2:
                        pe.wait_ge(s_d3, SCALE_STEPS * SUMS_BANKS.index(U1_BANKS[c]) + 1)
                    else:
                        pe.wait_ge(s_hid, c - 1)
                    pe.matmul(bank[U1_BANKS[c % 2]][:, 0:n], wc1[:, 0, :], x_t[:, c * COLS:c * COLS + n],
                              start=True, stop=False)

                def first_of_neighbours(c):
                    n = nodes_of(c)
                    pe.wait_ge(s_hs, 2 * (c + 1))
                    pe.matmul(bank[U1_BANKS[c % 2]][:, 0:n], wc1[:, 1, :], acc[:, 0, c * COLS:c * COLS + n],
                              start=False, stop=True).then_inc(s_u1, 1)

                def second(c):
                    pe.wait_ge(s_hid, c + 1)
                    if c < 2:
                        pe.wait_ge(s_pc3, len(loads))
                    else:
                        pe.wait_ge(s_y, c - 1)
                    for i in range(blocks_of(c)):
                        m = block_nodes(c * CHUNK + i)
                        last = pe.matmul(bank[U2_BANKS[c % 2]][0:m, i * P:(i + 1) * P],
                                         hidden[:, c % 2, i * P:i * P + m], wc2[:, :], start=True, stop=True)
                    last.then_inc(s_u2, 1)

                for n in range(3):
                    sums(n)
                scales(0)
                scales(1)
                broadcast(0)
                first_of_x(0)
                for b in range(2, len(loads)):
                    scales(b)
                    if b == 2:
                        broadcast(1)
                for c in range(n_chunks):
                    if c + 1 < n_chunks:
                        first_of_x(c + 1)
                    first_of_neighbours(c)
                    if c + 2 < n_chunks:
                        broadcast(c + 2)
                    if c >= 1:
                        second(c - 1)
                second(n_chunks - 1)

            @block.gpsimd
            def _(pool):
                for c in range(n_chunks):
                    cols = slice(c * COLS, c * COLS + nodes_of(c))
                    pool.wait_ge(s_sc, c + 1)
                    for k in range(1, HEADS):
                        if k > 1:
                            pool.wait_ge(s_hs, 2 * c + k - 1)
                        pool.tensor_tensor(acc[:, 0, cols], acc[:, 0, cols], acc[:, k, cols],
                                           ALU.add).then_inc(s_hs, 1)

            @block.scalar
            def _(act):
                def relu(c):
                    n = nodes_of(c)
                    act.wait_ge(s_u1, c + 1)
                    if c >= 2:
                        act.wait_ge(s_u2, c - 1)
                    act.activation(hidden[:, c % 2, 0:n], bank[U1_BANKS[c % 2]][:, 0:n], ACT.Relu,
                                   bias=bc1[:, 0:1]).then_inc(s_hid, 1)

                def deviations(c):
                    m, nb = min(nodes_of(c), P), blocks_of(c)
                    act.wait_ge(s_y, c + 1)
                    if c >= 1:
                        act.wait_ge(s_sq, c)
                    if c >= 3:
                        act.wait_ge(s_rec, c - 2)
                    for i in range(nb):
                        last = act.activation(square[0:m, i, :], y[0:m, c % 3, i, :], ACT.Square,
                                              accum_out=spread[0:m, c % 3, i:i + 1])
                    last.then_inc(s_sq, 1)
                    act.wait_ge(s_sq, c + 1)
                    act.activation(deviation[0:m, c % 3, 0:nb], spread[0:m, c % 3, 0:nb], ACT.Sqrt,
                                   bias=eps_col[0:m, 0:1], scale=1.0 / P).then_inc(s_dev, 1)

                for b, (_, blocks) in enumerate(loads):
                    act.wait_ge(s_pt3, b + 1)
                    act.copy(split[:, blocks[0] * P:(blocks[-1] + 1) * P],
                             bank_bf(LOAD_BANKS[b % 2])[0:3 * HEADS, 0:len(blocks) * P]).then_inc(s_pc3, 1)
                for c in range(n_chunks + 1):
                    if c < n_chunks:
                        relu(c)
                    if c >= 1:
                        deviations(c - 1)

            @block.vector
            def _(dve):
                chain = chained(dve, s_d3)

                def scales(n):
                    blocks = slice(stretches[n].start, stretches[n].stop)
                    some = per_node[:, blocks, :]
                    dve.wait_ge(s_at, n + 1)
                    chain(dve.tensor_scalar_max(
                        some, bank[SUMS_BANKS[n]][:, blocks.start * 4:blocks.stop * 4].rearrange(
                            "p (i j) -> p i j", j=4), 1.0))
                    chain(dve.reciprocal(some, some))
                    chain(dve.scalar_tensor_tensor(
                        some[:, :, 0:HEADS], some[:, :, 0:HEADS], 1.0 / HEADS,
                        some[:, :, HEADS:HEADS + 1].to_broadcast([P, len(stretches[n]), HEADS]),
                        ALU.mult, ALU.mult))
                    split_parts(dve, chain, blocks)

                def scale(c):
                    cols = slice(c * COLS, c * COLS + nodes_of(c))
                    dve.wait_ge(s_bs, c + 1)
                    for k in range(HEADS):
                        last = dve.tensor_tensor(acc[:, k, cols], acc[:, k, cols],
                                                 bank[HEAD_BANKS[k]][:, 0:nodes_of(c)], ALU.mult)
                    last.then_inc(s_sc, 1)

                def residual(c):
                    m, nb = min(nodes_of(c), P), blocks_of(c)
                    dve.wait_ge(s_u2, c + 1)
                    if c >= 3:
                        dve.wait_ge(s_sq, c - 2)
                        dve.wait_ge(s_res, c - 2)
                    dve.tensor_tensor(y[0:m, c % 3, 0:nb, :],
                                      bank[U2_BANKS[c % 2]][0:m, 0:nb * P].rearrange("p (i f) -> p i f", f=P),
                                      x_rows[0:m, c * CHUNK:c * CHUNK + nb, :], ALU.add).then_inc(s_y, 1)

                def normalise(c):
                    m, nb = min(nodes_of(c), P), blocks_of(c)
                    dve.wait_ge(s_dev, c + 1)
                    dve.reciprocal(deviation[0:m, c % 3, 0:nb],
                                   deviation[0:m, c % 3, 0:nb]).then_inc(s_rec, 1)
                    dve.wait_ge(s_rec, c + 1)
                    if c >= 3:
                        dve.wait_ge(s_out[c % 3], 16 * (c // 3))
                    dve.tensor_tensor(res[0:m, c % 3, 0:nb, :], y[0:m, c % 3, 0:nb, :],
                                      deviation[0:m, c % 3, 0:nb].unsqueeze(2).to_broadcast([m, nb, P]),
                                      ALU.mult).then_inc(s_res, 1)

                for n in range(3):
                    scales(n)
                scale(0)
                scale(1)
                for c in range(n_chunks + 2):
                    if c + 2 < n_chunks:
                        scale(c + 2)
                    if 0 <= c - 1 < n_chunks:
                        residual(c - 1)
                    if 0 <= c - 2 < n_chunks:
                        normalise(c - 2)

            @block.sync
            def _(sp):
                for c in range(n_chunks):
                    n = nodes_of(c)
                    sp.wait_ge(s_res, c + 1)
                    if n == COLS:
                        to = out[c * COLS:(c + 1) * COLS, :].rearrange("(i p) f -> p i f", p=P)
                        of = res[:, c % 3, :, :]
                    else:
                        to, of = out[c * COLS:n_nodes, :], res[0:n, c % 3, 0, :]
                    sp.dma_start(to, of).then_inc(s_out[c % 3], 16)
                for j in range(3):
                    sp.wait_ge(s_out[j], 16 * len(range(j, n_chunks, 3)))


_INS = ["x", "src", "dst",
        "L0_gnn_W_msg_1", "L0_gnn_W_msg_2", "L0_gnn_W_msg_3", "L0_gnn_b_msg_1", "L0_gnn_b_msg_2", "L0_gnn_b_msg_3",
        "L0_gnn_W_att_1", "L0_gnn_W_att_2", "L0_gnn_W_att_3", "L0_gnn_b_att_1", "L0_gnn_b_att_2", "L0_gnn_b_att_3",
        "L0_gnn_W_c1", "L0_gnn_b_c1", "L0_gnn_W_c2", "L0_gnn_b_c2"]


def kernel(**inputs):
    import numpy as np
    import concourse.bacc as bacc
    from concourse.bass_utils import run_bass_kernel_spmd

    nc = bacc.Bacc("TRN2", target_bir_lowering=False, num_devices=1)
    arrays, a = {}, {}
    for name in _INS:
        v = np.ascontiguousarray(inputs[name])
        arrays[f"in_{name}"] = v
        a[name.replace("L0_gnn_", "")] = nc.dram_tensor(
            f"in_{name}", v.shape, mybir.dt.from_np(v.dtype), kind="ExternalInput").ap()
    n, d = inputs["x"].shape
    table = nc.dram_tensor("message_table", (n, ROW), mybir.dt.float32, kind="Internal").ap()
    out = nc.dram_tensor("out", (n, d), mybir.dt.float32, kind="ExternalOutput").ap()
    gnn_program(nc, a["x"], a["src"], a["dst"], [a[f"W_msg_{k}"] for k in (1, 2, 3)],
                [a[f"b_msg_{k}"] for k in (1, 2, 3)], [a[f"W_att_{k}"] for k in (1, 2, 3)],
                [a[f"b_att_{k}"] for k in (1, 2, 3)], a["W_c1"], a["b_c1"], a["W_c2"], a["b_c2"], table, out)
    r = run_bass_kernel_spmd(nc, [arrays], core_ids=[0])
    return r.results[0]["out"]
```

```python
import concourse.bass as bass
import concourse.mybir as mybir
from contextlib import ExitStack

P = 128
HEADS = 3
WIN = 48
TILES = 2
GROUP = TILES * P
ROW = P + HEADS
CHUNK = 4
COLS = CHUNK * P
DONE = float(1 << 20)
FLT_MAX = 3.4028234663852886e38
EPS = 1e-5

EARLY = 14
RING = 6
N_EXP = 3
N_WT = 3
N_SUM = 3
N_QW = 2
REGS = 16
STEP = 2


def gnn_program(nc, x, src, dst, w_msg, b_msg, w_att, b_att, w_c1, b_c1, w_c2, b_c2, table, out):
    f32, bf16, i32 = mybir.dt.float32, mybir.dt.bfloat16, mybir.dt.int32
    ALU, ACT, AX = mybir.AluOpType, mybir.ActivationFunctionType, mybir.AxisListType.X

    n_nodes = x.shape[0]
    n_edges = src.shape[0]
    n_blocks = -(-n_nodes // P)
    n_cols = n_blocks * P
    n_pad = -(-max(n_cols, n_nodes + WIN) // 32) * 32
    n_chunks = -(-n_blocks // CHUNK)
    n_groups = -(-n_edges // GROUP)
    n_rows = -(-n_groups // P)
    full_groups = n_edges // GROUP
    tail_edges = n_edges - full_groups * GROUP
    pair = CHUNK // TILES
    n_early = EARLY * pair
    assert n_early <= min(P, full_groups)

    def blocks_of(c):
        return min(CHUNK, n_blocks - c * CHUNK)

    def nodes_of(c):
        return min(COLS, n_nodes - c * COLS)

    def block_nodes(i):
        return min(P, n_nodes - i * P)

    def tile_edges(g, h):
        return min(P, n_edges - g * GROUP - h * P)

    ctx = ExitStack()
    with ctx:
        def sb(name, shape, dt=f32):
            return ctx.enter_context(nc.sbuf_tensor(name, shape, dt))

        def sem(name):
            return ctx.enter_context(nc.semaphore(name))

        early = sb("early", [P, EARLY * CHUNK, ROW])
        assert n_chunks <= EARLY
        x_rows = early[:, :, :].rearrange("p t r -> p (t r)")[:, 0:n_blocks * P].rearrange(
            "p (i f) -> p i f", f=P)
        x_t = sb("x_t", [P, n_cols])
        acc = sb("acc", [P, HEADS + 1, n_pad])
        split = sb("split", [3 * HEADS, n_pad], bf16)
        w1 = sb("w1", [P, P])
        w2 = sb("w2", [P, P])
        w3 = sb("w3", [P, P])
        wc1 = sb("wc1", [P, 2, P])
        wc2 = sb("wc2", [P, P])
        w_logit = sb("w_logit", [P, 2 * HEADS])
        b1 = sb("b1", [P, 1])
        b2 = sb("b2", [P, 1])
        bc1 = sb("bc1", [P, 1])
        b3_all = sb("b3_all", [P, P])
        bc2_all = sb("bc2_all", [P, P])
        b_logit = sb("b_logit", [P, HEADS])
        ident = sb("ident", [P, P])
        ident_bf = sb("ident_bf", [P, P], bf16)
        pick = sb("pick", [3 * HEADS, HEADS, P], bf16)
        columns = sb("columns", [P, WIN])
        columns_i = sb("columns_i", [P, WIN], i32)
        per_node = sb("per_node", [P, n_blocks, 4])
        part_rest = sb("part_rest", [P, n_blocks, HEADS])
        parts = sb("parts", [P, n_blocks, 3 * HEADS], bf16)
        eps_col = sb("eps_col", [P, 1])
        zero_col = sb("zero_col", [P, 1])
        wc2_sum = sb("wc2_sum", [P, 1])
        x_sum = sb("x_sum", [P, CHUNK])

        n_ids = 2 * n_rows * GROUP
        ids_i = acc[:, HEADS, 0:n_ids].bitcast(i32).rearrange("p (j r e) -> p j r e", j=2, e=GROUP)
        dst_left = sb("dst_left", [P, n_rows, GROUP])
        src_t = sb("src_t", [P, TILES, n_rows * P], i32)
        dst_t = sb("dst_t", [P, TILES, n_rows * P])
        win_row = sb("win_row", [1, n_rows * P], i32)
        win_col = sb("win_col", [P, n_rows])
        least = sb("least", [P, 1])
        least_all = sb("least_all", [1, 1])
        more = sb("more", [1, 1], i32)

        WORK = 5250
        work = sb("work", [P, WORK])

        def area(at, *dims):
            n = 1
            for d in dims:
                n *= d
            view = work[:, at:at + n]
            if len(dims) == 2:
                view = view.rearrange("p (a b) -> p a b", a=dims[0])
            if len(dims) == 3:
                view = view.rearrange("p (a b c) -> p a b c", a=dims[0], b=dims[1])
            if len(dims) == 4:
                view = view.rearrange("p (a b c d) -> p a b c d", a=dims[0], b=dims[1], c=dims[2])
            return view, at + n

        bank = [ctx.enter_context(nc.psum_tensor(f"bank{i}", [P, 512], f32)) for i in range(8)]

        def bank_bf(i):
            return bank[i][:, :].bitcast(bf16)

        h1, at = area(0, 2, COLS)
        h2, at = area(at, 2, COLS)
        src_f, _ = area(at, n_rows, GROUP)
        rows, at = area(at, 2, CHUNK, ROW)
        assert n_rows * GROUP <= 2 * CHUNK * ROW
        X_RING = 4
        acc_flat = acc[:, :, :].rearrange("p k n -> p (k n)")
        ids_at, zeros = HEADS * n_pad, 4 * n_pad
        act_share = zeros // (3 * n_chunks)
        dve_from = act_share * n_chunks
        dve_pieces = 4
        dve_share = -(-(zeros - dve_from) // (n_chunks * dve_pieces))
        assert dve_from + 3 * dve_pieces * dve_share <= ids_at
        x_in, at = area(at, X_RING, CHUNK, P)
        assert at <= WORK

        T_BANK, L1_BANK, L2_BANK, L3_BANK, LOGIT_BANK, PARTS_BANK = 0, 2, 3, 4, 6, 7
        IDS_BANKS = (1, PARTS_BANK)
        assert n_early <= P < n_groups
        src_parts = (slice(0, 1), slice(1, n_rows))
        n_id_dmas = (full_groups // P + (full_groups % P > 0) + (tail_edges > 0))

        s_wb = [sem(f"s_wb{j}") for j in range(3)]
        s_wl = sem("s_wl")
        s_wu = sem("s_wu")
        s_x = [sem(f"s_x{c}") for c in range(n_chunks)]
        s_src0 = sem("s_src0")
        s_ids = [sem("s_src_in"), sem("s_dst_in")]
        s_idz = sem("s_idz")
        s_const = sem("s_const")
        s_cdve = sem("s_cdve")
        s_tr = sem("s_tr")
        s_xt = sem("s_xt")
        s_l1 = sem("s_l1")
        s_h1 = sem("s_h1")
        s_l2 = sem("s_l2")
        s_h2 = sem("s_h2")
        s_l3 = sem("s_l3")
        s_msg = sem("s_msg")
        s_pq = sem("s_pq")
        s_row = sem("s_row")
        s_tab = [sem(f"s_tab{j}") for j in range(2)]
        s_split = sem("s_split")
        s_pt = sem("s_pt")
        s_pc = sem("s_pc")
        s_srcf = sem("s_srcf")
        s_srct = sem("s_srct")
        s_src = sem("s_src")
        s_dst = sem("s_dst")
        s_cen = sem("s_cen")
        s_early = sem("s_early")
        SPLIT_STEPS = 5

        def split_parts(dve, chain, blocks, fill=lambda step: None):
            value = per_node[:, blocks, 0:HEADS]
            for j in range(3):
                part = parts[:, blocks, j * HEADS:(j + 1) * HEADS]
                chain(dve.tensor_copy(part, value), lambda: fill(2 * j))
                if j < 2:
                    chain(dve.tensor_tensor(part_rest[:, blocks, :], value, part, ALU.subtract),
                          lambda: fill(2 * j + 1))
                    value = part_rest[:, blocks, :]

        def transpose_parts(pe, to, blocks):
            for i in blocks:
                at = (i - blocks[0]) * P
                last = pe.transpose(to[0:3 * HEADS, at:at + P], parts[:, i, :], ident_bf[:, :])
            return last

        def chained(eng, s):
            count = [0]

            def chain(instruction, between=lambda: None):
                count[0] += 1
                instruction.then_inc(s, 1)
                between()
                eng.wait_ge(s, count[0])
            return chain

        def column(v):
            return v.rearrange("(p o) -> p o", o=1)

        with nc.Block() as block:
            @block.sync
            def _(sp):
                def load_ids(j, ids, rows_of_ids, landed):
                    for r in rows_of_ids:
                        if r == n_rows - 1:
                            sp.wait_ge(s_idz, 2)
                        n = min(P, full_groups - r * P)
                        if n > 0:
                            sp.dma_start(ids_i[0:n, j, r, :],
                                         ids[r * P * GROUP:(r * P + n) * GROUP].rearrange("(p e) -> p e", e=GROUP)
                                         ).then_inc(landed, 16)
                        if tail_edges and r == full_groups // P:
                            p = full_groups % P
                            sp.dma_start(ids_i[p:p + 1, j, r, 0:tail_edges],
                                         ids[full_groups * GROUP:n_edges].rearrange("(p e) -> p e", p=1)
                                         ).then_inc(landed, 16)

                def load_x(c):
                    n = nodes_of(c)
                    if c >= X_RING:
                        sp.wait_ge(s_tr, c - X_RING + 1)
                    if n == COLS:
                        to = x_in[:, c % X_RING, :, :]
                        of = x[c * COLS:(c + 1) * COLS, :].rearrange("(i p) f -> p i f", p=P)
                    else:
                        assert n <= P
                        to, of = x_in[0:n, c % X_RING, 0, :], x[c * COLS:n_nodes, :]
                    sp.dma_start(to, of).then_inc(s_x[c], 16)

                def store_rows(c):
                    n = nodes_of(c)
                    sp.wait_ge(s_row, c + 1)
                    if n == COLS:
                        to = table[c * COLS:(c + 1) * COLS, :].rearrange("(i p) f -> p i f", p=P)
                        of = rows[:, c % 2, :, :]
                    else:
                        to, of = table[c * COLS:n_nodes, :], rows[0:n, c % 2, 0, :]
                    sp.dma_start(to, of).then_inc(s_tab[c % 2], 16)

                load_ids(0, src, range(1), s_src0)
                AHEAD = 7
                for c in range(n_chunks + AHEAD):
                    if c < n_chunks:
                        load_x(c)
                    if c == 1:
                        load_ids(0, src, range(1, n_rows), s_ids[0])
                    if c == 2:
                        sp.dma_start(w3[:, :], w_msg[2]).then_inc(s_wb[2], 16)
                        sp.dma_start(b3_all[:, :], b_msg[2].partition_broadcast(P)).then_inc(s_wb[2], 16)
                    if c == X_RING - 1:
                        for k in range(HEADS):
                            for h in range(2):
                                sp.dma_start(w_logit[:, h * HEADS + k:h * HEADS + k + 1],
                                             w_att[k][h * P:(h + 1) * P, :]).then_inc(s_wl, 16)
                            sp.dma_start(b_logit[:, k:k + 1], b_att[k].partition_broadcast(P)).then_inc(s_wl, 16)
                    if c == X_RING:
                        load_ids(1, dst, range(n_rows), s_ids[1])
                        for to, of in ((bc1[:, :], column(b_c1)), (bc2_all[:, :], b_c2.partition_broadcast(P)),
                                       (wc1[:, :, :], w_c1.rearrange("(h p) f -> p h f", p=P)),
                                       (wc2[:, :], w_c2)):
                            sp.dma_start(to, of).then_inc(s_wu, 16)
                    if c >= AHEAD:
                        store_rows(c - AHEAD)
                for j in range(2):
                    sp.wait_ge(s_tab[j], 16 * len(range(j, n_chunks, 2)))

            @block.scalar
            def _(act):
                for to, of, s in ((w1, w_msg[0], s_wb[0]), (b1, column(b_msg[0]), s_wb[0]),
                                  (w2, w_msg[1], s_wb[1]), (b2, column(b_msg[1]), s_wb[1])):
                    act.dma_start(to[:, :], of).then_inc(s, 16)
                act.wait_ge(s_const, 2)
                for c in range(n_chunks + 5):
                    if c < n_chunks:
                        a = c * act_share
                        act.copy(acc_flat[:, a:a + act_share], zero_col[:, 0:1].to_broadcast([P, act_share]))
                        n = nodes_of(c)
                        act.wait_ge(s_tr, c + 1)
                        act.copy(x_t[:, c * COLS:c * COLS + n], bank[T_BANK][:, 0:n]).then_inc(s_xt, 1)
                    if 1 <= c <= n_chunks:
                        n = nodes_of(c - 1)
                        act.wait_ge(s_l1, c)
                        if c == 1:
                            act.wait_ge(s_wb[0], 32)
                        if c >= 3:
                            act.wait_ge(s_l2, c - 2)
                        act.activation(h1[:, (c - 1) % 2, 0:n], bank[L1_BANK][:, 0:n], ACT.Relu,
                                       bias=b1[:, 0:1]).then_inc(s_h1, 1)
                    if 0 <= c - 4 < n_chunks:
                        d, nb, m = c - 4, blocks_of(c - 4), min(nodes_of(c - 4), P)
                        act.wait_ge(s_msg, d + 1)
                        act.activation(rows[0:m, d % 2, 0:nb, 0:P], rows[0:m, d % 2, 0:nb, 0:P],
                                       ACT.Relu).then_inc(s_row, 1)
                    if c >= 5:
                        d, n = c - 5, blocks_of(c - 5) * P
                        act.wait_ge(s_pt, d + 1)
                        act.copy(split[:, d * COLS:d * COLS + n],
                                 bank_bf(PARTS_BANK)[0:3 * HEADS, 0:n]).then_inc(s_pc, 1)

            @block.vector
            def _(dve):
                for j in range(2):
                    dve.memset(ids_i[:, j, n_rows - 1, :], int(DONE) * j).then_inc(s_idz, 1)
                chain = chained(dve, s_cdve)
                dve.memset(eps_col[:, :], EPS)
                dve.memset(split[:, n_cols:n_pad], 0.0)
                dve.memset(x_t[:, n_nodes:n_cols], 0.0)
                chain(dve.memset(per_node[:, :, :], 0.0))
                for n, rs in enumerate(src_parts):
                    if n == 0:
                        dve.wait_ge(s_src0, 16)
                    else:
                        dve.wait_ge(s_ids[0], 16 * (n_id_dmas - 1))
                    dve.tensor_copy(src_f[:, rs, :], ids_i[:, 0, rs, :]).then_inc(s_srcf, 1)
                    for h in range(TILES):
                        dve.wait_ge(s_srct, n * TILES + h + 1)
                        dve.tensor_copy(src_t[:, h, rs.start * P:rs.stop * P],
                                        bank[IDS_BANKS[h]][:, rs.start * P:rs.stop * P]).then_inc(s_src, 1)
                dve.wait_ge(s_const, 6)
                chain(dve.tensor_copy(ident_bf[:, :], ident[:, :]))
                chain(dve.tensor_copy(columns[:, :], columns_i[:, :]))

                def zero(piece):
                    at = dve_from + piece * dve_share
                    if at < zeros:
                        dve.memset(acc_flat[:, at:min(at + dve_share, zeros)], 0.0)

                dve.wait_ge(s_wb[1], 32)
                split_chain = chained(dve, s_split)
                for c in range(n_chunks + 1):
                    if c < n_chunks:
                        n = nodes_of(c)
                        dve.wait_ge(s_l2, c + 1)
                        if c >= 2:
                            dve.wait_ge(s_l3, c - 1)
                        dve.tensor_scalar(h2[:, c % 2, 0:n], bank[L2_BANK][:, 0:n], b2[:, 0:1], 0.0,
                                          ALU.add, ALU.max).then_inc(s_h2, 1)
                    if c == 0:
                        dve.wait_ge(s_wb[2], 32)
                        dve.wait_ge(s_wl, 16 * 3 * HEADS)
                    if c >= 1:
                        d = c - 1
                        nb, m = blocks_of(d), min(nodes_of(d), P)
                        mine = slice(d * CHUNK, d * CHUNK + nb)
                        dve.wait_ge(s_l3, d + 1)
                        if d >= 2:
                            dve.wait_ge(s_tab[d % 2], 16 * (d // 2))
                        logits = bank[LOGIT_BANK][0:m, 0:nb * 6].rearrange("p (i j) -> p i j", j=6)
                        dve.tensor_copy(rows[0:m, d % 2, 0:nb, P:ROW], logits[:, :, 0:HEADS])
                        dve.tensor_tensor(per_node[0:m, mine, 0:HEADS], logits[:, :, HEADS:2 * HEADS],
                                          b_logit[0:m, :].unsqueeze(1).to_broadcast([m, nb, HEADS]),
                                          ALU.add).then_inc(s_pq, 1)
                        dve.tensor_tensor(rows[0:m, d % 2, 0:nb, 0:P],
                                          bank[L3_BANK + d % 2][0:m, 0:nb * P].rearrange(
                                              "p (i f) -> p i f", f=P),
                                          b3_all[0:m, :].unsqueeze(1).to_broadcast([m, nb, P]),
                                          ALU.add).then_inc(s_msg, 1)
                        dve.wait_ge(s_pq, d + 1)
                        split_parts(dve, split_chain, mine,
                                    lambda step: zero(d * dve_pieces + step) if step < dve_pieces else None)
                    if c == 2:
                        dve.wait_ge(s_ids[1], 16 * n_id_dmas)
                        dve.tensor_copy(dst_left[:, :, :], ids_i[:, 1, :, :]).then_inc(s_dst, 1)
                        dve.wait_ge(s_dst, 1)
                    if c == 3:
                        dve.wait_ge(s_wu, 64)
                        centre = chained(dve, s_cen)
                        centre(dve.tensor_reduce(wc2_sum[:, :], wc2[:, :], AX, ALU.add))
                        centre(dve.scalar_tensor_tensor(wc2[:, :], wc2_sum[:, 0:1].to_broadcast([P, P]), -1.0 / P,
                                                        wc2[:, :], ALU.mult, ALU.add))
            @block.gpsimd
            def _(pool):
                pool.memset(ident[:, :], 0.0).then_inc(s_const, 1)
                pool.memset(zero_col[:, :], 0.0)
                pool.memset(pick[:, :, :], 0.0).then_inc(s_const, 1)
                pool.iota(columns_i[:, :], pattern=[[1, WIN]], base=0,
                          channel_multiplier=0).then_inc(s_const, 1)
                pool.wait_ge(s_const, 3)
                pool.affine_select(out=ident[:, :], in_=ident[:, :], compare_op=ALU.not_equal, fill=1.0,
                                   base=0, pattern=[[-1, P]], channel_multiplier=1).then_inc(s_const, 1)
                for part in range(3):
                    pool.affine_select(out=pick[:, :, :], in_=pick[:, :, :], compare_op=ALU.not_equal,
                                       fill=1.0, base=-HEADS * part, pattern=[[-1, HEADS], [0, P]],
                                       channel_multiplier=1).then_inc(s_const, 1)
                    pool.wait_ge(s_const, 5 + part)
                pool.wait_ge(s_src, TILES)
                for t in range(EARLY * CHUNK):
                    g, h = t // TILES, t % TILES
                    pool.indirect_dma_start(
                        out=early[:, t, 0:P], out_offset=None, in_=x[:, :],
                        in_offset=bass.IndirectOffsetOnAxis(ap=src_t[:, h, g:g + 1], axis=0),
                    ).then_inc(s_early, 16)

            @block.tensor
            def _(pe):
                pe.wait_ge(s_const, 4)

                def transpose_src(n):
                    pe.wait_ge(s_srcf, n + 1)
                    pe.wait_ge(s_src, n * TILES)
                    for h in range(TILES):
                        for r in range(n_rows)[src_parts[n]]:
                            last = pe.transpose(bank[IDS_BANKS[h]][:, r * P:(r + 1) * P],
                                                src_f[:, r, h * P:(h + 1) * P], ident[:, :])
                        last.then_inc(s_srct, 1)

                transpose_src(0)
                for s in range(n_chunks + 5):
                    if s < n_chunks:
                        c = s
                        pe.wait_ge(s_x[c], 16)
                        if c >= 1:
                            pe.wait_ge(s_xt, c)
                        for i in range(blocks_of(c)):
                            m = block_nodes(c * CHUNK + i)
                            last = pe.transpose(bank[T_BANK][:, i * P:i * P + m],
                                                x_in[0:m, c % X_RING, i, :], ident[0:m, 0:m])
                        last.then_inc(s_tr, 1)
                    if 0 <= s - 1 < n_chunks:
                        c, n = s - 1, nodes_of(s - 1)
                        if c == 0:
                            pe.wait_ge(s_wb[0], 32)
                        pe.wait_ge(s_xt, c + 1)
                        if c >= 1:
                            pe.wait_ge(s_h1, c)
                        pe.matmul(bank[L1_BANK][:, 0:n], w1[:, :], x_t[:, c * COLS:c * COLS + n],
                                  start=True, stop=True).then_inc(s_l1, 1)
                    if s == 1:
                        transpose_src(1)
                    if 0 <= s - 2 < n_chunks:
                        c, n = s - 2, nodes_of(s - 2)
                        if c == 0:
                            pe.wait_ge(s_wb[1], 32)
                        pe.wait_ge(s_h1, c + 1)
                        if c >= 1:
                            pe.wait_ge(s_h2, c)
                        pe.matmul(bank[L2_BANK][:, 0:n], w2[:, :], h1[:, c % 2, 0:n],
                                  start=True, stop=True).then_inc(s_l2, 1)
                    if 0 <= s - 5 < n_chunks:
                        c = s - 5
                        if c == 0:
                            pe.wait_ge(s_cdve, 2)
                        pe.wait_ge(s_split, SPLIT_STEPS * (c + 1))
                        if c >= 1:
                            pe.wait_ge(s_pc, c)
                        transpose_parts(pe, bank_bf(PARTS_BANK),
                                        range(c * CHUNK, c * CHUNK + blocks_of(c))).then_inc(s_pt, 1)
                    if 0 <= s - 3 < n_chunks:
                        c = s - 3
                        if c == 0:
                            pe.wait_ge(s_wb[2], 32)
                            pe.wait_ge(s_wl, 16 * 3 * HEADS)
                        pe.wait_ge(s_h2, c + 1)
                        if c >= 1:
                            pe.wait_ge(s_pq, c)
                        if c >= 2:
                            pe.wait_ge(s_msg, c - 1)
                        for i in range(blocks_of(c)):
                            b = c * CHUNK + i
                            m = block_nodes(b)
                            pe.matmul(bank[L3_BANK + c % 2][0:m, i * P:(i + 1) * P],
                                      h2[:, c % 2, i * P:i * P + m], w3[:, :], start=True, stop=True)
                            last = pe.matmul(bank[LOGIT_BANK][0:m, i * 6:(i + 1) * 6],
                                             x_t[:, b * P:b * P + m], w_logit[:, :], start=True, stop=True)
                        last.then_inc(s_l3, 1)

        nc.all_engine_barrier()

        gath, at = area(0, RING * TILES, ROW)
        dist, at2 = area(at, n_rows, GROUP)
        assert at2 <= WORK
        expo, at = area(at, N_EXP, HEADS + 1, TILES * WIN)
        mask, at = area(at, N_EXP, TILES, WIN)
        wt, at = area(at, N_WT, HEADS + 1, TILES * WIN)
        a_sum, at = area(at, N_WT, TILES, HEADS + 1)
        hit, at2 = area(at, n_rows, GROUP)
        assert at2 <= WORK
        early_x, at = area(at, 1, COLS)
        early_h, at = area(at, 1, COLS)
        assert at <= WORK

        EARLY_BANKS = (5, 6, 7)

        EARLY_STAGES = 6
        between = (n_groups - n_early) // EARLY
        FIRST_STAGE = 10
        lead = FIRST_STAGE + STEP * EARLY_STAGES
        assert between >= lead
        first_order = []
        starts = {}
        for e in range(EARLY):
            others = range(n_early + e * between, n_early + (e + 1) * between)
            starts[e] = len(first_order) + FIRST_STAGE
            first_order += others[:lead]
            for g in range(e * pair, (e + 1) * pair):
                first_order.append(g)
            first_order += others[lead:]
        first_order += range(n_early + EARLY * between, n_groups)
        LEFT_STEPS, LEFT_PE, LEFT_END = (4, 5, 6, 7), 8, 9
        assert LEFT_END < FIRST_STAGE
        early_done = [first_order.index((e + 1) * pair - 1) for e in range(EARLY)]

        s_xr = [sem(f"s_xr{c}") for c in range(n_chunks)]
        s_first = sem("s_first")
        s_prep = sem("s_prep")
        s_ptr = sem("s_ptr")
        s_left = sem("s_left")
        s_least = sem("s_least")
        s_gath = [sem(f"s_gath{j}") for j in range(RING * TILES)]
        s_fill = sem("s_fill")
        s_qw = sem("s_qw")
        s_exp = sem("s_exp")
        s_mask = sem("s_mask")
        s_wt = sem("s_wt")
        s_as = sem("s_as")
        s_sum = sem("s_sum")
        s_acc = sem("s_acc")
        s_last = sem("s_last")

        def edge_pass(first):
            order = first_order if first else list(range(n_groups))
            n_own = n_early if first else 0
            others = [g for g in order if g >= n_own]
            turn = {g: n for n, g in enumerate(others)}
            position = {g: i for i, g in enumerate(order)}

            def rows_of(g, h):
                return early[:, g * TILES + h, :] if g < n_own else gath[:, (turn[g] % RING) * TILES + h, :]

            def rows_landed(eng, g, h):
                if g < n_own:
                    eng.wait_ge(s_row, n_chunks + g // pair + 1)
                else:
                    eng.wait_ge(s_gath[(turn[g] % RING) * TILES + h], 16 * (turn[g] // RING + 1))

            def stages(i):
                return [(e, (i - at) // STEP) for e, at in starts.items()
                        if first and i >= at and (i - at) % STEP == 0 and (i - at) // STEP < EARLY_STAGES]

            def window_registers(eng):
                regs = {}

                def window(g):
                    if g not in regs:
                        n = min(pair, n_own - g) if g < n_own else min(REGS, n_groups - g)
                        fresh = [eng.alloc_register(f"win{first}_{g + j}") for j in range(n)]
                        eng.load(fresh, win_row[0:1, g:g + n])
                        for j in range(n):
                            regs[g + j] = eng.snap(fresh[j], donate=True, min_val=0, max_val=n_nodes)
                    return regs.pop(g)
                return window

            with nc.Block() as block:
                @block.gpsimd
                def _(pool):
                    for n, g in enumerate(others):
                        if n >= RING:
                            pool.wait_ge(s_sum, position[others[n - RING]] + 1)
                        for h in range(TILES):
                            m = tile_edges(g, h)
                            slot = (n % RING) * TILES + h
                            pool.indirect_dma_start(
                                out=gath[0:m, slot, :], out_offset=None, in_=table[:, :],
                                in_offset=bass.IndirectOffsetOnAxis(ap=src_t[0:m, h, g:g + 1], axis=0),
                            ).then_inc(s_gath[slot], 16)
                    for j in range(RING * TILES):
                        pool.wait_ge(s_gath[j], 16 * len(range(j // TILES, len(others), RING)))

                if first:
                    @block.sync
                    def _(sp):
                        for c in range(n_chunks):
                            n = nodes_of(c)
                            sp.wait_ge(s_sum, early_done[c] + 1)
                            if n == COLS:
                                to = x_rows[:, c * CHUNK:(c + 1) * CHUNK, :]
                                of = x[c * COLS:(c + 1) * COLS, :].rearrange("(i p) f -> p i f", p=P)
                            else:
                                to, of = x_rows[0:n, c * CHUNK, :], x[c * COLS:n_nodes, :]
                            sp.dma_start(to, of).then_inc(s_xr[c], 16)

                @block.tensor
                def _(pe):
                    even, odd, logits = (bank[b] for b in EARLY_BANKS)
                    pe.wait_ge(s_prep, 2)
                    for r in range(n_rows):
                        last = pe.transpose(even[0:1, r * P:(r + 1) * P], win_col[:, r:r + 1], ident[:, :])
                    last.then_inc(s_ptr, 1)
                    pe.wait_ge(s_prep, 3)
                    for h in range(TILES):
                        for r in range(n_rows):
                            last = pe.transpose(bank[h][:, r * P:(r + 1) * P],
                                                dist[:, r, h * P:(h + 1) * P], ident[:, :])
                        last.then_inc(s_ptr, 1)
                    pe.wait_ge(s_prep, 4 + TILES)
                    window = window_registers(pe)

                    def q_window(i):
                        start = window(order[i])
                        if i >= N_QW:
                            pe.wait_ge(s_exp, i - N_QW + 1)
                        for k in range(HEADS):
                            last = pe.matmul(bank[i % N_QW][:, k * WIN:(k + 1) * WIN], pick[:, k, :],
                                             split[:, bass.ds(start, WIN)], start=True, stop=True)
                        last.then_inc(s_qw, 1)

                    def early_stage(e, stage):
                        c = n_chunks + e
                        tiles = range(e * CHUNK, (e + 1) * CHUNK)
                        if stage == 0:
                            if e == 0:
                                pe.wait_ge(s_early, 16 * EARLY * CHUNK)
                            pe.wait_ge(s_h2, c)
                            for i, t in enumerate(tiles):
                                last = pe.transpose(even[:, i * P:(i + 1) * P], early[:, t, 0:P], ident[:, :])
                            last.then_inc(s_tr, 1)
                        elif stage == 1:
                            pe.wait_ge(s_xt, c + 1)
                            pe.wait_ge(s_msg, c)
                            pe.matmul(odd[:, :], w1[:, :], early_x[:, 0, :],
                                      start=True, stop=True).then_inc(s_l1, 1)
                        elif stage == 2:
                            pe.wait_ge(s_h1, c + 1)
                            pe.matmul(even[:, :], w2[:, :], early_h[:, 0, :],
                                      start=True, stop=True).then_inc(s_l2, 1)
                        elif stage == 3:
                            pe.wait_ge(s_left, len(LEFT_STEPS) + 1)
                            pe.wait_ge(s_h2, c + 1)
                            for i in range(CHUNK):
                                cols = slice(i * P, (i + 1) * P)
                                pe.matmul(odd[:, cols], early_h[:, 0, cols], w3[:, :], start=True, stop=True)
                                last = pe.matmul(logits[:, i * HEADS:(i + 1) * HEADS], early_x[:, 0, cols],
                                                 w_logit[:, 0:HEADS], start=True, stop=True)
                            last.then_inc(s_l3, 1)

                    for i in range(N_QW):
                        q_window(i)
                    pe.wait_ge(s_fill, 1)
                    for i, g in enumerate(order):
                        sums = bank[N_QW + i % N_SUM]
                        tiles = [h for h in range(TILES) if tile_edges(g, h) > 0]
                        pe.wait_ge(s_wt, i + 1)
                        if i >= N_SUM:
                            pe.wait_ge(s_acc, i - N_SUM + 1)
                        for h in tiles:
                            m = tile_edges(g, h)
                            rows_landed(pe, g, h)
                            pe.matmul(sums[:, 0:HEADS * WIN], rows_of(g, h)[0:m, 0:P],
                                      wt[0:m, i % N_WT, 0:HEADS, h * WIN:(h + 1) * WIN],
                                      start=h == tiles[0], stop=h == tiles[-1])
                        pe.wait_ge(s_as, i + 1)
                        for h in tiles:
                            m = tile_edges(g, h)
                            last = pe.matmul(sums[0:HEADS + 1, HEADS * WIN:(HEADS + 1) * WIN],
                                             a_sum[0:m, i % N_WT, h, :],
                                             wt[0:m, i % N_WT, HEADS, h * WIN:(h + 1) * WIN],
                                             start=h == tiles[0], stop=h == tiles[-1])
                        last.then_inc(s_sum, 1)
                        if i + N_QW < n_groups:
                            q_window(i + N_QW)
                        if i == LEFT_PE:
                            pe.wait_ge(s_left, len(LEFT_STEPS))
                            pe.transpose(logits[0:1, 0:P], least[:, :], ident[:, :]).then_inc(s_least, 1)
                        for e, stage in stages(i):
                            early_stage(e, stage)

                @block.scalar
                def _(act):
                    def early_stage(e, stage):
                        c = n_chunks + e
                        even, odd, _ = (bank[b] for b in EARLY_BANKS)
                        mine = slice(e * CHUNK, (e + 1) * CHUNK)
                        if stage == 1:
                            act.wait_ge(s_tr, c + 1)
                            act.wait_ge(s_left, len(LEFT_STEPS))
                            act.wait_ge(s_l3, c)
                            act.copy(early_x[:, 0, :], even[:, :]).then_inc(s_xt, 1)
                        elif stage == 2:
                            act.wait_ge(s_l1, c + 1)
                            act.activation(early_h[:, 0, :], odd[:, :], ACT.Relu,
                                           bias=b1[:, 0:1]).then_inc(s_h1, 1)
                        elif stage == 5:
                            act.wait_ge(s_msg, c + 1)
                            act.activation(early[:, mine, 0:P], early[:, mine, 0:P], ACT.Relu).then_inc(s_row, 1)

                    for i, g in enumerate(order):
                        for e, stage in stages(i):
                            early_stage(e, stage)
                        act.wait_ge(s_qw, i + 1)
                        if i >= N_EXP:
                            act.wait_ge(s_wt, i - N_EXP + 1)
                        for h in range(TILES):
                            m = tile_edges(g, h)
                            rows_landed(act, g, h)
                            for k in range(HEADS):
                                last = act.activation(expo[0:m, i % N_EXP, k, h * WIN:(h + 1) * WIN],
                                                      bank[i % N_QW][0:m, k * WIN:(k + 1) * WIN], ACT.Exp,
                                                      bias=rows_of(g, h)[0:m, P + k:P + k + 1])
                        last.then_inc(s_exp, 1)

                @block.vector
                def _(dve):
                    chain = chained(dve, s_prep)
                    chain(dve.tensor_reduce(win_col[:, :], dst_left[:, :, :], AX, ALU.min))
                    chain(dve.tensor_scalar_min(win_col[:, :], win_col[:, :], float(n_nodes)))
                    chain(dve.tensor_tensor(dist[:, :, :], dst_left[:, :, :],
                                            win_col[:, :].unsqueeze(2).to_broadcast([P, n_rows, GROUP]),
                                            ALU.subtract))
                    dve.wait_ge(s_ptr, 1)
                    chain(dve.tensor_copy(win_row[0:1, :], bank[EARLY_BANKS[0]][0:1, 0:n_rows * P]))
                    dve.memset(a_sum[:, :, :, :], 1.0)
                    for j in range(N_SUM):
                        dve.memset(bank[N_QW + j][:, HEADS * WIN:(HEADS + 1) * WIN], 0.0)
                    for h in range(TILES):
                        dve.wait_ge(s_ptr, 2 + h)
                        chain(dve.tensor_copy(dst_t[:, h, :], bank[h][:, 0:n_rows * P]))
                    for j in range(N_EXP):
                        last = dve.memset(expo[:, j, HEADS, :], 0.0)
                    last.then_inc(s_fill, 1)
                    dve.wait_ge(s_fill, 1)

                    def left(step):
                        dve.wait_ge(s_left, step)
                        if step == 0:
                            last = dve.tensor_tensor(hit[:, :, :], dst_left[:, :, :],
                                                     win_col[:, :].unsqueeze(2).to_broadcast([P, n_rows, GROUP]),
                                                     ALU.subtract)
                        elif step == 1:
                            last = dve.tensor_scalar(hit[:, :, :], hit[:, :, :], float(WIN), DONE,
                                                     ALU.is_lt, ALU.mult)
                        elif step == 2:
                            last = dve.tensor_tensor(dst_left[:, :, :], dst_left[:, :, :], hit[:, :, :], ALU.add)
                        else:
                            last = dve.tensor_reduce(least[:, :], dst_left[:, :, :].rearrange("p r e -> p (r e)"),
                                                     AX, ALU.min)
                        last.then_inc(s_left, 1)

                    def another_pass():
                        dve.wait_ge(s_least, 1)
                        dve.tensor_reduce(least_all[:, :], bank[EARLY_BANKS[2]][0:1, 0:P], AX,
                                          ALU.min).then_inc(s_left, 1)
                        dve.wait_ge(s_left, len(LEFT_STEPS) + 1)
                        dve.tensor_scalar(more[:, :], least_all[:, :], DONE, None, ALU.is_lt).then_inc(s_left, 1)

                    window = window_registers(dve)

                    def masks(i):
                        g = order[i]
                        if i >= N_EXP:
                            dve.wait_ge(s_wt, i - N_EXP + 1)
                        for h in range(TILES):
                            last = dve.tensor_scalar(mask[:, i % N_EXP, h, :], columns[:, :],
                                                     dst_t[:, h, g:g + 1], FLT_MAX, ALU.is_equal, ALU.mult)
                        last.then_inc(s_mask, 1)

                    def add_sums(i):
                        start = window(order[i])
                        dve.wait_ge(s_sum, i + 1)
                        if i >= 1:
                            dve.wait_ge(s_acc, i)
                        here = acc[:, :, bass.ds(start, WIN)]
                        dve.tensor_tensor(here, here,
                                          bank[N_QW + i % N_SUM][:, 0:(HEADS + 1) * WIN].rearrange(
                                              "p (k w) -> p k w", w=WIN), ALU.add).then_inc(s_acc, 1)

                    def early_stage(e, stage):
                        c = n_chunks + e
                        even, odd, logits = (bank[b] for b in EARLY_BANKS)
                        mine = slice(e * CHUNK, (e + 1) * CHUNK)
                        if stage == 3:
                            dve.wait_ge(s_l2, c + 1)
                            dve.tensor_scalar(early_h[:, 0, :], even[:, :], b2[:, 0:1], 0.0,
                                              ALU.add, ALU.max).then_inc(s_h2, 1)
                        elif stage == 4:
                            dve.wait_ge(s_l3, c + 1)
                            dve.tensor_copy(early[:, mine, P:ROW], logits[:, 0:CHUNK * HEADS].rearrange(
                                "p (i k) -> p i k", k=HEADS))
                            dve.tensor_tensor(early[:, mine, 0:P],
                                              odd[:, :].rearrange("p (i f) -> p i f", f=P),
                                              b3_all[:, :].unsqueeze(1).to_broadcast([P, CHUNK, P]),
                                              ALU.add).then_inc(s_msg, 1)

                    def centre_x(c, step):
                        m, nb = min(nodes_of(c), P), blocks_of(c)
                        here = x_rows[0:m, c * CHUNK:c * CHUNK + nb, :]
                        dve.wait_ge(s_cen, 2 + 3 * c + step)
                        if step == 0:
                            dve.wait_ge(s_xr[c], 16)
                            last = dve.tensor_tensor(here, here, bc2_all[0:m, :].unsqueeze(1).to_broadcast(
                                [m, nb, P]), ALU.add)
                        elif step == 1:
                            last = dve.tensor_reduce(x_sum[0:m, 0:nb], here, AX, ALU.add)
                        else:
                            last = dve.scalar_tensor_tensor(
                                here, x_sum[0:m, 0:nb].unsqueeze(2).to_broadcast([m, nb, P]), -1.0 / P,
                                here, ALU.mult, ALU.add)
                        last.then_inc(s_cen, 1)

                    centre_at = {early_done[c] + STEP + 2 + step: (c, step)
                                 for c in range(n_chunks) for step in range(3)} if first else {}
                    masks(0)
                    for i, g in enumerate(order):
                        if i + 1 < n_groups:
                            masks(i + 1)
                        dve.wait_ge(s_exp, i + 1)
                        dve.wait_ge(s_mask, i + 1)
                        if i >= N_WT:
                            dve.wait_ge(s_sum, i - N_WT + 1)
                        both = mask[:, i % N_EXP, :, :].rearrange("p h w -> p (h w)")
                        dve.scalar_tensor_tensor(wt[:, i % N_WT, :, :], expo[:, i % N_EXP, :, :], 1.0,
                                                 both.unsqueeze(1).to_broadcast([P, HEADS + 1, TILES * WIN]),
                                                 ALU.max, ALU.min).then_inc(s_wt, 1)
                        if i >= 1:
                            add_sums(i - 1)
                        dve.wait_ge(s_wt, i + 1)
                        dve.tensor_reduce(
                            a_sum[:, i % N_WT, :, 0:HEADS].rearrange("p h k -> p k h"),
                            wt[:, i % N_WT, 0:HEADS, :].rearrange("p k (h w) -> p k h w", h=TILES),
                            AX, ALU.add).then_inc(s_as, 1)
                        for e, stage in stages(i):
                            early_stage(e, stage)
                        if i in LEFT_STEPS:
                            left(LEFT_STEPS.index(i))
                        if i == LEFT_END:
                            another_pass()
                        if i in centre_at:
                            centre_x(*centre_at[i])
                    add_sums(n_groups - 1)

        more_reg = nc.alloc_registers("more")

        def branch():
            nc.regs_load(more_reg, more[0:1, 0:1])
            nc.br_cmp(more_reg, 0, on_true="pass_end", on_false="pass_again", comp_op="IS_EQ",
                      engines=mybir.ALL_ENGINES)

        edge_pass(first=True)
        branch()
        with nc.body("pass_again", valid_engines=mybir.ALL_ENGINES):
            nc.gpsimd.dma_reset(range(s_first.num, s_last.num + 1))
            nc.all_engine_barrier(sems_to_clear=range(s_first.num, s_last.num + 1))
            edge_pass(first=False)
            branch()
        nc.switch_bb("pass_end")

        hidden, at = area(0, 2, COLS)
        y, at = area(at, 3, CHUNK, P)
        res, at = area(at, 3, CHUNK, P)
        square, at = area(at, CHUNK, P)
        spread, at = area(at, 3, CHUNK)
        deviation, at = area(at, 3, CHUNK)
        assert at <= WORK

        SCALE_STEPS = 3 + SPLIT_STEPS
        ends = [min(c, n_chunks) for c in (1, 3, 7, n_chunks)]
        stretches = [range(a * CHUNK, min(b * CHUNK, n_blocks)) for a, b in zip([0] + ends, ends)]
        HEAD_BANKS, U1_BANKS, U2_BANKS, PARTS_BANK = (0, 1, 2), (3, 4), (5, 6), 7
        SUMS_BANKS = (PARTS_BANK, U1_BANKS[1], U2_BANKS[0], U2_BANKS[1])

        def stretch_of(c):
            return next(n for n, end in enumerate(ends) if c < end)

        s_at = sem("s_at")
        s_d3 = sem("s_d3")
        s_pt3 = sem("s_pt3")
        s_pc3 = sem("s_pc3")
        s_bs = sem("s_bs")
        s_sc = sem("s_sc")
        s_hs = sem("s_hs")
        s_u1 = sem("s_u1")
        s_hid = sem("s_hid")
        s_u2 = sem("s_u2")
        s_y = sem("s_y")
        s_sq = sem("s_sq")
        s_dev = sem("s_dev")
        s_rec = sem("s_rec")
        s_res = sem("s_res")
        s_out = [sem(f"s_out{j}") for j in range(3)]

        with nc.Block() as block:
            @block.tensor
            def _(pe):
                def sums(n):
                    for i in stretches[n]:
                        last = pe.transpose(bank[SUMS_BANKS[n]][:, i * 4:(i + 1) * 4],
                                            acc[0:4, HEADS, i * P:(i + 1) * P], ident[0:4, 0:4])
                    last.then_inc(s_at, 1)

                def wait_sums_read(b):
                    if b in SUMS_BANKS:
                        pe.wait_ge(s_d3, SCALE_STEPS * SUMS_BANKS.index(b) + 1)

                def scales(c):
                    pe.wait_ge(s_d3, SCALE_STEPS * (stretch_of(c) + 1))
                    if c >= 1:
                        pe.wait_ge(s_pc3, c)
                    transpose_parts(pe, bank_bf(PARTS_BANK),
                                    range(c * CHUNK, c * CHUNK + blocks_of(c))).then_inc(s_pt3, 1)

                def broadcast(c):
                    if c >= 1:
                        pe.wait_ge(s_sc, c)
                    pe.wait_ge(s_pc3, c + 1)
                    n = nodes_of(c)
                    for k in range(HEADS):
                        last = pe.matmul(bank[HEAD_BANKS[k]][:, 0:n], pick[:, k, :],
                                         split[:, c * COLS:c * COLS + n], start=True, stop=True)
                    last.then_inc(s_bs, 1)

                def first_of_x(c):
                    n = nodes_of(c)
                    if c < 2:
                        wait_sums_read(U1_BANKS[c])
                    else:
                        pe.wait_ge(s_hid, c - 1)
                    pe.matmul(bank[U1_BANKS[c % 2]][:, 0:n], wc1[:, 0, :], x_t[:, c * COLS:c * COLS + n],
                              start=True, stop=False)

                def first_of_neighbours(c):
                    n = nodes_of(c)
                    pe.wait_ge(s_hs, 2 * (c + 1))
                    pe.matmul(bank[U1_BANKS[c % 2]][:, 0:n], wc1[:, 1, :], acc[:, 0, c * COLS:c * COLS + n],
                              start=False, stop=True).then_inc(s_u1, 1)

                def second(c):
                    pe.wait_ge(s_hid, c + 1)
                    if c < 2:
                        wait_sums_read(U2_BANKS[c])
                    else:
                        pe.wait_ge(s_y, c - 1)
                    for i in range(blocks_of(c)):
                        m = block_nodes(c * CHUNK + i)
                        last = pe.matmul(bank[U2_BANKS[c % 2]][0:m, i * P:(i + 1) * P],
                                         hidden[:, c % 2, i * P:i * P + m], wc2[:, :], start=True, stop=True)
                    last.then_inc(s_u2, 1)

                sums(0)
                sums(1)
                scales(0)
                sums(2)
                broadcast(0)
                scales(1)
                first_of_x(0)
                first_of_x(1)
                scales(2)
                broadcast(1)
                for c in range(n_chunks):
                    if 1 <= c and c + 2 < n_chunks:
                        broadcast(c + 2)
                    if 1 <= c and c + 3 < n_chunks:
                        scales(c + 3)
                    if c >= 1:
                        second(c - 1)
                    first_of_neighbours(c)
                    if c == 0:
                        broadcast(2)
                        scales(3)
                        sums(3)
                    elif c + 1 < n_chunks:
                        first_of_x(c + 1)
                second(n_chunks - 1)

            @block.gpsimd
            def _(pool):
                for c in range(n_chunks):
                    cols = slice(c * COLS, c * COLS + nodes_of(c))
                    pool.wait_ge(s_sc, c + 1)
                    for k in range(1, HEADS):
                        if k > 1:
                            pool.wait_ge(s_hs, 2 * c + k - 1)
                        pool.tensor_tensor(acc[:, 0, cols], acc[:, 0, cols], acc[:, k, cols],
                                           ALU.add).then_inc(s_hs, 1)

            @block.scalar
            def _(act):
                def relu(c):
                    n = nodes_of(c)
                    act.wait_ge(s_u1, c + 1)
                    if c >= 2:
                        act.wait_ge(s_u2, c - 1)
                    act.activation(hidden[:, c % 2, 0:n], bank[U1_BANKS[c % 2]][:, 0:n], ACT.Relu,
                                   bias=bc1[:, 0:1]).then_inc(s_hid, 1)

                def deviations(c):
                    m, nb = min(nodes_of(c), P), blocks_of(c)
                    act.wait_ge(s_y, c + 1)
                    if c >= 1:
                        act.wait_ge(s_sq, c)
                    if c >= 3:
                        act.wait_ge(s_rec, c - 2)
                    for i in range(nb):
                        last = act.activation(square[0:m, i, :], y[0:m, c % 3, i, :], ACT.Square,
                                              accum_out=spread[0:m, c % 3, i:i + 1])
                    last.then_inc(s_sq, 1)
                    act.wait_ge(s_sq, c + 1)
                    act.activation(deviation[0:m, c % 3, 0:nb], spread[0:m, c % 3, 0:nb], ACT.Sqrt,
                                   bias=eps_col[0:m, 0:1], scale=1.0 / P).then_inc(s_dev, 1)

                def copy_scales(c):
                    n = blocks_of(c) * P
                    act.wait_ge(s_pt3, c + 1)
                    act.copy(split[:, c * COLS:c * COLS + n],
                             bank_bf(PARTS_BANK)[0:3 * HEADS, 0:n]).then_inc(s_pc3, 1)

                for c in range(3):
                    copy_scales(c)
                for c in range(n_chunks + 1):
                    if 1 <= c and c + 3 < n_chunks:
                        copy_scales(c + 3)
                    if c < n_chunks:
                        relu(c)
                    if c == 0:
                        copy_scales(3)
                    if c >= 1:
                        deviations(c - 1)

            @block.vector
            def _(dve):
                chain = chained(dve, s_d3)

                def scales(n):
                    blocks = slice(stretches[n].start, stretches[n].stop)
                    some = per_node[:, blocks, :]
                    dve.wait_ge(s_at, n + 1)
                    chain(dve.tensor_scalar_max(
                        some, bank[SUMS_BANKS[n]][:, blocks.start * 4:blocks.stop * 4].rearrange(
                            "p (i j) -> p i j", j=4), 1.0))
                    chain(dve.reciprocal(some, some))
                    chain(dve.scalar_tensor_tensor(
                        some[:, :, 0:HEADS], some[:, :, 0:HEADS], 1.0 / HEADS,
                        some[:, :, HEADS:HEADS + 1].to_broadcast([P, len(stretches[n]), HEADS]),
                        ALU.mult, ALU.mult))
                    split_parts(dve, chain, blocks)

                def scale(c):
                    cols = slice(c * COLS, c * COLS + nodes_of(c))
                    dve.wait_ge(s_bs, c + 1)
                    for k in range(HEADS):
                        last = dve.tensor_tensor(acc[:, k, cols], acc[:, k, cols],
                                                 bank[HEAD_BANKS[k]][:, 0:nodes_of(c)], ALU.mult)
                    last.then_inc(s_sc, 1)

                def residual(c):
                    m, nb = min(nodes_of(c), P), blocks_of(c)
                    dve.wait_ge(s_u2, c + 1)
                    if c >= 3:
                        dve.wait_ge(s_sq, c - 2)
                        dve.wait_ge(s_res, c - 2)
                    dve.tensor_tensor(y[0:m, c % 3, 0:nb, :],
                                      bank[U2_BANKS[c % 2]][0:m, 0:nb * P].rearrange("p (i f) -> p i f", f=P),
                                      x_rows[0:m, c * CHUNK:c * CHUNK + nb, :], ALU.add).then_inc(s_y, 1)

                def normalise(c):
                    m, nb = min(nodes_of(c), P), blocks_of(c)
                    dve.wait_ge(s_dev, c + 1)
                    dve.reciprocal(deviation[0:m, c % 3, 0:nb],
                                   deviation[0:m, c % 3, 0:nb]).then_inc(s_rec, 1)
                    dve.wait_ge(s_rec, c + 1)
                    if c >= 3:
                        dve.wait_ge(s_out[c % 3], 16 * (c // 3))
                    dve.tensor_tensor(res[0:m, c % 3, 0:nb, :], y[0:m, c % 3, 0:nb, :],
                                      deviation[0:m, c % 3, 0:nb].unsqueeze(2).to_broadcast([m, nb, P]),
                                      ALU.mult).then_inc(s_res, 1)

                scales(0)
                scales(1)
                scale(0)
                scales(2)
                scale(1)
                for c in range(n_chunks + 2):
                    if c + 2 < n_chunks:
                        scale(c + 2)
                    if c == 0:
                        scales(3)
                    if 0 <= c - 1 < n_chunks:
                        residual(c - 1)
                    if 0 <= c - 2 < n_chunks:
                        normalise(c - 2)

            @block.sync
            def _(sp):
                for c in range(n_chunks):
                    n = nodes_of(c)
                    sp.wait_ge(s_res, c + 1)
                    if n == COLS:
                        to = out[c * COLS:(c + 1) * COLS, :].rearrange("(i p) f -> p i f", p=P)
                        of = res[:, c % 3, :, :]
                    else:
                        to, of = out[c * COLS:n_nodes, :], res[0:n, c % 3, 0, :]
                    sp.dma_start(to, of).then_inc(s_out[c % 3], 16)
                for j in range(3):
                    sp.wait_ge(s_out[j], 16 * len(range(j, n_chunks, 3)))


_INS = ["x", "src", "dst",
        "L0_gnn_W_msg_1", "L0_gnn_W_msg_2", "L0_gnn_W_msg_3", "L0_gnn_b_msg_1", "L0_gnn_b_msg_2", "L0_gnn_b_msg_3",
        "L0_gnn_W_att_1", "L0_gnn_W_att_2", "L0_gnn_W_att_3", "L0_gnn_b_att_1", "L0_gnn_b_att_2", "L0_gnn_b_att_3",
        "L0_gnn_W_c1", "L0_gnn_b_c1", "L0_gnn_W_c2", "L0_gnn_b_c2"]


def kernel(**inputs):
    import numpy as np
    import concourse.bacc as bacc
    from concourse.bass_utils import run_bass_kernel_spmd

    nc = bacc.Bacc("TRN2", target_bir_lowering=False, num_devices=1)
    arrays, a = {}, {}
    for name in _INS:
        v = np.ascontiguousarray(inputs[name])
        arrays[f"in_{name}"] = v
        a[name.replace("L0_gnn_", "")] = nc.dram_tensor(
            f"in_{name}", v.shape, mybir.dt.from_np(v.dtype), kind="ExternalInput").ap()
    n, d = inputs["x"].shape
    table = nc.dram_tensor("message_table", (n, ROW), mybir.dt.float32, kind="Internal").ap()
    out = nc.dram_tensor("out", (n, d), mybir.dt.float32, kind="ExternalOutput").ap()
    gnn_program(nc, a["x"], a["src"], a["dst"], [a[f"W_msg_{k}"] for k in (1, 2, 3)],
                [a[f"b_msg_{k}"] for k in (1, 2, 3)], [a[f"W_att_{k}"] for k in (1, 2, 3)],
                [a[f"b_att_{k}"] for k in (1, 2, 3)], a["W_c1"], a["b_c1"], a["W_c2"], a["b_c2"], table, out)
    r = run_bass_kernel_spmd(nc, [arrays], core_ids=[0])
    return r.results[0]["out"]
```
